# Optimizing a Trainium2 kernel written in Bass

```python
import numpy as np
import jax
import jax.numpy as jnp

def _softmax(x, axis=-1):
    return jax.nn.softmax(x, axis=axis)

def _gelu(x):
    return jax.nn.gelu(x, approximate=True)

def _silu(x):
    return jax.nn.silu(x)

def _sigmoid(x):
    return jax.nn.sigmoid(x)

def _layernorm(x, axis=-1, eps=1e-05):
    m = jnp.mean(x, axis=axis, keepdims=True)
    v = jnp.var(x, axis=axis, keepdims=True)
    return (x - m) / jnp.sqrt(v + eps)

def _scatter_add(tgt, idx, src, axis=0):
    return tgt.at[idx].add(src)

def _segment_sum(src, seg, n):
    return jax.ops.segment_sum(src, seg, n)
kernel_name = 'mk_gnn_ffn_d4_gnn_r32_2f7deb'

def setup_inputs(seed: int=0):
    np.random.seed(seed)
    _w = jnp.asarray

    def _rec_inputs():
        import jax
        import jax.numpy as jnp
        _gk = jax.random.key(seed)
        x = -8.776e-05 + 1 * jax.random.normal(jax.random.fold_in(_gk, 1), (625, 256), jnp.float32)
        src = jax.random.randint(jax.random.fold_in(_gk, 2), (10000,), 0, 625, jnp.int32)
        dst = jax.random.randint(jax.random.fold_in(_gk, 3), (10000,), 0, 625, jnp.int32)
        _o = jnp.argsort(dst, stable=True)
        src = src[_o]
        dst = dst[_o]
        edge_type_2 = jax.random.randint(jax.random.fold_in(_gk, 13), (10000,), 0, 2, jnp.int32)
        return (x, src, dst, edge_type_2)
    x, src, dst, edge_type_2 = _rec_inputs()

    def _L0_gnn_setup():
        import jax, jax.numpy as jnp
        import numpy as np
        N_NODES = 625
        key = jax.random.key(seed)
        k1, k2, k3, k4 = jax.random.split(key, 4)
        d = 256
        E = 10000
        x = jax.random.normal(k1, (N_NODES, d), dtype=jnp.float32)
        edge_index = jax.random.randint(k2, (2, E), 0, N_NODES, dtype=jnp.int64)
        limit = float(np.sqrt(6.0 / (d + d)))
        W_l = jax.random.uniform(k3, (d, d), dtype=jnp.float32, minval=-limit, maxval=limit)
        W_r = jax.random.uniform(k4, (d, d), dtype=jnp.float32, minval=-limit, maxval=limit)
        b_r = jnp.zeros((d,), dtype=jnp.float32)
        return {'x': x, 'edge_index': edge_index, 'W_l': W_l, 'W_r': W_r, 'b_r': b_r}
    _L0_gnn_all = _L0_gnn_setup()
    _L0_gnn_in = {k: v for k, v in _L0_gnn_all.items() if k in ('W_l', 'W_r', 'b_r')}
    del _L0_gnn_all

    def _L0_ffn_setup():
        import jax, jax.numpy as jnp
        import numpy as np
        B, T, C = (64, 384, 256)
        NH, NKV = (4, 2)
        HD = C // NH
        NREP = NH // NKV
        NE, TOPK = (8, 2)
        HID = int(8 / 3 * C)
        EPS_RMS = 1e-06

        def _rope_tables(t_len):
            inv_freq = 1.0 / 10000.0 ** (np.arange(0, HD, 2, dtype=np.float32) / HD)
            t = np.arange(t_len, dtype=np.float32)
            freqs = np.outer(t, inv_freq)
            emb = np.concatenate([freqs, freqs], axis=-1)
            return (jnp.asarray(np.cos(emb)), jnp.asarray(np.sin(emb)))

        def _rotate_half(x):
            h = x.shape[-1] // 2
            return jnp.concatenate([-x[..., h:], x[..., :h]], axis=-1)

        def _rmsnorm(v, w):
            return v * jax.lax.rsqrt(jnp.mean(v * v, axis=-1, keepdims=True) + EPS_RMS) * w
        key = jax.random.key(seed)
        ks = jax.random.split(key, 10)
        s = lambda k, shape: jax.random.normal(k, shape, jnp.float32) * 0.02
        return {'x': jax.random.normal(ks[0], (B, T, C), jnp.float32), 'ln1_w': jnp.ones((C,), jnp.float32), 'ln2_w': jnp.ones((C,), jnp.float32), 'wq': s(ks[1], (NH * HD, C)), 'wk': s(ks[2], (NKV * HD, C)), 'wv': s(ks[3], (NKV * HD, C)), 'wo': s(ks[4], (C, C)), 'router_w': s(ks[5], (NE, C)), 'w1': s(ks[6], (NE, HID, C)), 'w2': s(ks[7], (NE, C, HID)), 'w3': s(ks[8], (NE, HID, C))}
    _L0_ffn_all = _L0_ffn_setup()
    _L0_ffn_in = {k: v for k, v in _L0_ffn_all.items() if k in ('ln1_w', 'ln2_w', 'wq', 'wk', 'wv', 'wo', 'router_w', 'w1', 'w2', 'w3')}
    del _L0_ffn_all

    def _L1_gnn_setup():
        import jax, jax.numpy as jnp
        import numpy as np
        N_NODES = 10000
        N_EDGES = 10000
        D = 256
        D_OUT = 256
        NUM_REL = 2
        key = jax.random.key(seed)
        ks = jax.random.split(key, 16)
        s = 1.0 / np.sqrt(D)
        inp = {}
        inp['feat'] = jax.random.normal(ks[0], (N_NODES, D), dtype=jnp.float32)
        inp['src'] = jax.random.randint(ks[1], (N_EDGES,), 0, N_NODES, dtype=jnp.int32)
        inp['dst'] = jax.random.randint(ks[2], (N_EDGES,), 0, N_NODES, dtype=jnp.int32)
        inp['rel'] = jax.random.randint(ks[3], (N_EDGES,), 0, NUM_REL, dtype=jnp.int32)
        inp['W_rel'] = jax.random.normal(ks[4], (NUM_REL, D, D), dtype=jnp.float32) * s
        inp['b_rel'] = jax.random.normal(ks[5], (NUM_REL, D), dtype=jnp.float32) * s
        inp['W_ih'] = jax.random.normal(ks[6], (4 * D, D), dtype=jnp.float32) * s
        inp['b_ih'] = jax.random.normal(ks[7], (4 * D,), dtype=jnp.float32) * s
        inp['b_hh'] = jax.random.normal(ks[8], (4 * D,), dtype=jnp.float32) * s
        h = D // 2
        inp['W1'] = jax.random.normal(ks[9], (h, D), dtype=jnp.float32) * s
        inp['b1'] = jax.random.normal(ks[10], (h,), dtype=jnp.float32) * s
        inp['W2'] = jax.random.normal(ks[11], (h, h), dtype=jnp.float32) * (1.0 / np.sqrt(h))
        inp['b2'] = jax.random.normal(ks[12], (h,), dtype=jnp.float32) * (1.0 / np.sqrt(h))
        inp['W3'] = jax.random.normal(ks[13], (D_OUT, h), dtype=jnp.float32) * (1.0 / np.sqrt(h))
        inp['b3'] = jax.random.normal(ks[14], (D_OUT,), dtype=jnp.float32) * (1.0 / np.sqrt(h))
        return inp
    _L1_gnn_all = _L1_gnn_setup()
    _L1_gnn_in = {k: v for k, v in _L1_gnn_all.items() if k in ('W_rel', 'b_rel', 'W_ih', 'b_ih', 'b_hh', 'W1', 'b1', 'W2', 'b2', 'W3', 'b3')}
    del _L1_gnn_all

    def _L1_ffn_setup():
        import jax, jax.numpy as jnp
        import numpy as np
        E = 8
        K = 2
        D = 256
        H = 512
        DOUT = 256
        EPS = 1e-05
        key = jax.random.key(seed)
        ks = jax.random.split(key, 9)
        s = 0.02
        return {'x': jax.random.normal(ks[0], (4, 256, D), jnp.float32), 'gamma': 1.0 + 0.05 * jax.random.normal(ks[1], (D,), jnp.float32), 'beta': 0.05 * jax.random.normal(ks[2], (D,), jnp.float32), 'Wr': 0.01 * jax.random.normal(ks[3], (D, E), jnp.float32), 'br': jnp.zeros((E,), jnp.float32), 'W1': s * jax.random.normal(ks[4], (E, D, H), jnp.float32), 'b1': s * jax.random.normal(ks[5], (E, H), jnp.float32), 'W2': s * jax.random.normal(ks[6], (E, H, DOUT), jnp.float32), 'b2': s * jax.random.normal(ks[7], (E, DOUT), jnp.float32)}
    _L1_ffn_all = _L1_ffn_setup()
    _L1_ffn_in = {k: v for k, v in _L1_ffn_all.items() if k in ('gamma', 'beta', 'Wr', 'br', 'W1', 'b1', 'W2', 'b2')}
    del _L1_ffn_all

    def _L2_gnn_setup():
        import jax, jax.numpy as jnp
        import numpy as np
        N_NODES = 50000
        N_EDGES = 25000
        DIM = 256
        NUM_HEADS = 8
        key = jax.random.key(seed)
        k_x, k_wu, k_bu, k_wv, k_src, k_dst = jax.random.split(key, 6)
        x = jax.random.normal(k_x, (N_NODES, DIM), dtype=jnp.float32)
        W_u = jax.random.normal(k_wu, (NUM_HEADS, DIM), dtype=jnp.float32) * (1.0 / np.sqrt(DIM))
        b_u = jax.random.normal(k_bu, (NUM_HEADS,), dtype=jnp.float32) * 0.01
        W_v = jax.random.normal(k_wv, (NUM_HEADS, DIM), dtype=jnp.float32) * (1.0 / np.sqrt(DIM))
        src = jax.random.randint(k_src, (N_EDGES,), 0, N_NODES, dtype=jnp.int32)
        dst = jax.random.randint(k_dst, (N_EDGES,), 0, N_NODES, dtype=jnp.int32)
        return {'x': x, 'W_u': W_u, 'b_u': b_u, 'W_v': W_v, 'src': src, 'dst': dst}
    _L2_gnn_all = _L2_gnn_setup()
    _L2_gnn_in = {k: v for k, v in _L2_gnn_all.items() if k in ('W_u', 'b_u', 'W_v')}
    del _L2_gnn_all

    def _L2_ffn_setup():
        import jax, jax.numpy as jnp
        import numpy as np
        NUM_EXPERTS = 8
        TOP_K = 2
        B, S, D = (8, 256, 256)

        def _moe(tokens, router_w, w1, b1, w2, b2):
            N = tokens.shape[0]
            E = router_w.shape[0]
            logits = tokens.astype(jnp.float32) @ router_w.astype(jnp.float32).T
            probs = jax.nn.softmax(logits, axis=-1)
            rw, re = jax.lax.top_k(probs, TOP_K)
            if TOP_K > 1:
                rw = rw / jnp.maximum(rw.sum(-1, keepdims=True), 1e-12)
            rw = rw.astype(tokens.dtype)
            combine = jnp.zeros((N, E), tokens.dtype).at[jnp.arange(N)[:, None], re].set(rw)
            out = tokens
            for e in range(E):
                h = jax.nn.gelu(tokens @ w1[e] + b1[e], approximate=False)
                y = h @ w2[e] + b2[e]
                out = out + combine[:, e:e + 1] * y
            return out
        key = jax.random.key(seed)
        ks = jax.random.split(key, 4)
        scale = 1.0 / np.sqrt(D).astype(np.float32)
        return {'input_embeddings': jax.random.normal(ks[0], (B, S, D), jnp.float32), 'router_w': jax.random.normal(ks[1], (NUM_EXPERTS, D), jnp.float32) * scale, 'w1': jax.random.normal(ks[2], (NUM_EXPERTS, D, D), jnp.float32) * scale, 'b1': jnp.zeros((NUM_EXPERTS, D), jnp.float32), 'w2': jax.random.normal(ks[3], (NUM_EXPERTS, D, D), jnp.float32) * scale, 'b2': jnp.zeros((NUM_EXPERTS, D), jnp.float32)}
    _L2_ffn_all = _L2_ffn_setup()
    _L2_ffn_in = {k: v for k, v in _L2_ffn_all.items() if k in ('router_w', 'w1', 'b1', 'w2', 'b2')}
    del _L2_ffn_all

    def _L3_gnn_setup():
        import jax, jax.numpy as jnp
        import numpy as np
        import math
        HIDDEN = 256
        DEPTH = 3
        RATIOS = (0.5, 0.5, 0.5)
        N = 625
        E = 10000

        def _sage_layer(x_src, x_dst, src, dst, emask, Wl, Wr, b):
            n_dst = x_dst.shape[0]
            msgs = x_src[src] * emask[:, None]
            s = jax.ops.segment_sum(msgs, dst, num_segments=n_dst)
            c = jax.ops.segment_sum(emask, dst, num_segments=n_dst)
            agg = s / jnp.maximum(c, 1.0)[:, None]
            return agg @ Wl.T + x_dst @ Wr.T + b

        def _cummean_pad(x_small, n_dst):
            n, d = x_small.shape
            cm = jnp.cumsum(x_small, axis=0) / jnp.arange(1, n + 1, dtype=x_small.dtype)[:, None]
            return jnp.concatenate([cm, jnp.zeros((n_dst - n, d), x_small.dtype)], axis=0)

        def _forward(x, edge_index, dWl1, dWr1, db1, dWl2, dWr2, db2, pool_w, uWl1, uWr1, ub1, uWl2, uWr2, ub2):
            src, dst = (edge_index[0], edge_index[1])
            emask = jnp.ones((src.shape[0],), x.dtype)
            xs = []
            n = x.shape[0]
            for i in range(DEPTH):
                xs.append(x)
                h = jax.nn.relu(_sage_layer(x, x, src, dst, emask, dWl1[i], dWr1[i], db1[i]))
                x = _sage_layer(h, h, src, dst, emask, dWl2[i], dWr2[i], db2[i])
                w_ = pool_w[i]
                score = jnp.tanh(x @ w_ / jnp.linalg.norm(w_))
                k = int(math.ceil(RATIOS[i] * n))
                vals, perm = jax.lax.top_k(score, k)
                x = x[perm] * vals[:, None]
                new_id = jnp.full((n,), -1, jnp.int32).at[perm].set(jnp.arange(k, dtype=jnp.int32))
                s2, d2 = (new_id[src], new_id[dst])
                emask = emask * (s2 >= 0).astype(x.dtype) * (d2 >= 0).astype(x.dtype)
                src, dst = (jnp.maximum(s2, 0), jnp.maximum(d2, 0))
                n = k
            for i in range(DEPTH - 2, -1, -1):
                skip = xs[i]
                n_src, n_dst = (x.shape[0], skip.shape[0])
                agg1 = _cummean_pad(x, n_dst)
                h = jax.nn.relu(agg1 @ uWl1[i].T + skip @ uWr1[i].T + ub1[i])
                agg2 = _cummean_pad(h[:n_src], n_dst)
                x = agg2 @ uWl2[i].T + h @ uWr2[i].T + ub2[i]
            return x
        key = jax.random.key(seed)
        ks = jax.random.split(key, 16)
        sc = 1.0 / np.sqrt(HIDDEN)

        def w(k, shape):
            return jax.random.normal(k, shape, jnp.float32) * sc
        return {'x': jax.random.normal(ks[0], (N, HIDDEN), jnp.float32), 'edge_index': jax.random.randint(ks[1], (2, E), 0, N, jnp.int32), 'dWl1': w(ks[2], (DEPTH, HIDDEN, HIDDEN)), 'dWr1': w(ks[3], (DEPTH, HIDDEN, HIDDEN)), 'db1': jnp.zeros((DEPTH, HIDDEN), jnp.float32), 'dWl2': w(ks[4], (DEPTH, HIDDEN, HIDDEN)), 'dWr2': w(ks[5], (DEPTH, HIDDEN, HIDDEN)), 'db2': jnp.zeros((DEPTH, HIDDEN), jnp.float32), 'pool_w': w(ks[6], (DEPTH, HIDDEN)), 'uWl1': w(ks[7], (DEPTH - 1, HIDDEN, HIDDEN)), 'uWr1': w(ks[8], (DEPTH - 1, HIDDEN, HIDDEN)), 'ub1': jnp.zeros((DEPTH - 1, HIDDEN), jnp.float32), 'uWl2': w(ks[9], (DEPTH - 1, HIDDEN, HIDDEN)), 'uWr2': w(ks[10], (DEPTH - 1, HIDDEN, HIDDEN)), 'ub2': jnp.zeros((DEPTH - 1, HIDDEN), jnp.float32)}
    _L3_gnn_all = _L3_gnn_setup()
    _L3_gnn_in = {k: v for k, v in _L3_gnn_all.items() if k in ('dWl1', 'dWr1', 'db1', 'dWl2', 'dWr2', 'db2', 'pool_w', 'uWl1', 'uWr1', 'ub1', 'uWl2', 'uWr2', 'ub2')}
    del _L3_gnn_all

    def _L3_ffn_setup():
        import jax, jax.numpy as jnp
        import numpy as np
        C = 256
        HID = 1024
        E = 8
        TEMP = 1.0
        key = jax.random.key(seed)
        ks = jax.random.split(key, 7)
        x = jax.random.normal(ks[0], (8, 512, C), dtype=jnp.float32)
        W1 = jax.random.normal(ks[1], (C, HID), dtype=jnp.float32) * 0.02
        b1 = jnp.zeros((HID,), dtype=jnp.float32)
        Wg = jax.random.normal(ks[2], (HID, E), dtype=jnp.float32) * 0.02
        bg = jnp.zeros((E,), dtype=jnp.float32)
        Wd = jax.random.normal(ks[3], (E, HID, C), dtype=jnp.float32) * 0.02
        bd = jnp.zeros((E, C), dtype=jnp.float32)
        return {'x': x, 'W1': W1, 'b1': b1, 'Wg': Wg, 'bg': bg, 'Wd': Wd, 'bd': bd}
    _L3_ffn_all = _L3_ffn_setup()
    _L3_ffn_in = {k: v for k, v in _L3_ffn_all.items() if k in ('W1', 'b1', 'Wg', 'bg', 'Wd', 'bd')}
    del _L3_ffn_all
    return {'x': x, 'src': src, 'dst': dst, 'edge_type_2': edge_type_2, 'L0_gnn_W_l': _L0_gnn_in['W_l'], 'L0_gnn_W_r': _L0_gnn_in['W_r'], 'L0_gnn_b_r': _L0_gnn_in['b_r'], 'L0_ffn_ln1_w': _L0_ffn_in['ln1_w'], 'L0_ffn_ln2_w': _L0_ffn_in['ln2_w'], 'L0_ffn_wq': _L0_ffn_in['wq'], 'L0_ffn_wk': _L0_ffn_in['wk'], 'L0_ffn_wv': _L0_ffn_in['wv'], 'L0_ffn_wo': _L0_ffn_in['wo'], 'L0_ffn_router_w': _L0_ffn_in['router_w'], 'L0_ffn_w1': _L0_ffn_in['w1'], 'L0_ffn_w2': _L0_ffn_in['w2'], 'L0_ffn_w3': _L0_ffn_in['w3'], 'L1_gnn_W_rel': _L1_gnn_in['W_rel'], 'L1_gnn_b_rel': _L1_gnn_in['b_rel'], 'L1_gnn_W_ih': _L1_gnn_in['W_ih'], 'L1_gnn_b_ih': _L1_gnn_in['b_ih'], 'L1_gnn_b_hh': _L1_gnn_in['b_hh'], 'L1_gnn_W1': _L1_gnn_in['W1'], 'L1_gnn_b1': _L1_gnn_in['b1'], 'L1_gnn_W2': _L1_gnn_in['W2'], 'L1_gnn_b2': _L1_gnn_in['b2'], 'L1_gnn_W3': _L1_gnn_in['W3'], 'L1_gnn_b3': _L1_gnn_in['b3'], 'L1_ffn_gamma': _L1_ffn_in['gamma'], 'L1_ffn_beta': _L1_ffn_in['beta'], 'L1_ffn_Wr': _L1_ffn_in['Wr'], 'L1_ffn_br': _L1_ffn_in['br'], 'L1_ffn_W1': _L1_ffn_in['W1'], 'L1_ffn_b1': _L1_ffn_in['b1'], 'L1_ffn_W2': _L1_ffn_in['W2'], 'L1_ffn_b2': _L1_ffn_in['b2'], 'L2_gnn_W_u': _L2_gnn_in['W_u'], 'L2_gnn_b_u': _L2_gnn_in['b_u'], 'L2_gnn_W_v': _L2_gnn_in['W_v'], 'L2_ffn_router_w': _L2_ffn_in['router_w'], 'L2_ffn_w1': _L2_ffn_in['w1'], 'L2_ffn_b1': _L2_ffn_in['b1'], 'L2_ffn_w2': _L2_ffn_in['w2'], 'L2_ffn_b2': _L2_ffn_in['b2'], 'L3_gnn_dWl1': _L3_gnn_in['dWl1'], 'L3_gnn_dWr1': _L3_gnn_in['dWr1'], 'L3_gnn_db1': _L3_gnn_in['db1'], 'L3_gnn_dWl2': _L3_gnn_in['dWl2'], 'L3_gnn_dWr2': _L3_gnn_in['dWr2'], 'L3_gnn_db2': _L3_gnn_in['db2'], 'L3_gnn_pool_w': _L3_gnn_in['pool_w'], 'L3_gnn_uWl1': _L3_gnn_in['uWl1'], 'L3_gnn_uWr1': _L3_gnn_in['uWr1'], 'L3_gnn_ub1': _L3_gnn_in['ub1'], 'L3_gnn_uWl2': _L3_gnn_in['uWl2'], 'L3_gnn_uWr2': _L3_gnn_in['uWr2'], 'L3_gnn_ub2': _L3_gnn_in['ub2'], 'L3_ffn_W1': _L3_ffn_in['W1'], 'L3_ffn_b1': _L3_ffn_in['b1'], 'L3_ffn_Wg': _L3_ffn_in['Wg'], 'L3_ffn_bg': _L3_ffn_in['bg'], 'L3_ffn_Wd': _L3_ffn_in['Wd'], 'L3_ffn_bd': _L3_ffn_in['bd']}

def reference(x, src, dst, edge_type_2, L0_gnn_W_l, L0_gnn_W_r, L0_gnn_b_r, L0_ffn_ln1_w, L0_ffn_ln2_w, L0_ffn_wq, L0_ffn_wk, L0_ffn_wv, L0_ffn_wo, L0_ffn_router_w, L0_ffn_w1, L0_ffn_w2, L0_ffn_w3, L1_gnn_W_rel, L1_gnn_b_rel, L1_gnn_W_ih, L1_gnn_b_ih, L1_gnn_b_hh, L1_gnn_W1, L1_gnn_b1, L1_gnn_W2, L1_gnn_b2, L1_gnn_W3, L1_gnn_b3, L1_ffn_gamma, L1_ffn_beta, L1_ffn_Wr, L1_ffn_br, L1_ffn_W1, L1_ffn_b1, L1_ffn_W2, L1_ffn_b2, L2_gnn_W_u, L2_gnn_b_u, L2_gnn_W_v, L2_ffn_router_w, L2_ffn_w1, L2_ffn_b1, L2_ffn_w2, L2_ffn_b2, L3_gnn_dWl1, L3_gnn_dWr1, L3_gnn_db1, L3_gnn_dWl2, L3_gnn_dWr2, L3_gnn_db2, L3_gnn_pool_w, L3_gnn_uWl1, L3_gnn_uWr1, L3_gnn_ub1, L3_gnn_uWl2, L3_gnn_uWr2, L3_gnn_ub2, L3_ffn_W1, L3_ffn_b1, L3_ffn_Wg, L3_ffn_bg, L3_ffn_Wd, L3_ffn_bd):
    import jax
    import jax.numpy as jnp

    def _L0_gnn_ref(x, edge_index, W_l, W_r, b_r):
        import jax, jax.numpy as jnp
        import numpy as np
        N_NODES = 625
        src, dst = (edge_index[0], edge_index[1])
        messages = x[src]
        sums = jax.ops.segment_sum(messages, dst, num_segments=N_NODES)
        counts = jax.ops.segment_sum(jnp.ones_like(dst, dtype=x.dtype), dst, num_segments=N_NODES)
        aggr = sums / jnp.maximum(counts, 1.0)[:, None]
        out = aggr @ W_l.T + x @ W_r.T + b_r
        return out

    def _L0_ffn_ref(x, ln1_w, ln2_w, wq, wk, wv, wo, router_w, w1, w2, w3):
        import jax, jax.numpy as jnp
        import numpy as np
        B, T, C = (64, 384, 256)
        NH, NKV = (4, 2)
        HD = C // NH
        NREP = NH // NKV
        NE, TOPK = (8, 2)
        HID = int(8 / 3 * C)
        EPS_RMS = 1e-06

        def _rope_tables(t_len):
            inv_freq = 1.0 / 10000.0 ** (np.arange(0, HD, 2, dtype=np.float32) / HD)
            t = np.arange(t_len, dtype=np.float32)
            freqs = np.outer(t, inv_freq)
            emb = np.concatenate([freqs, freqs], axis=-1)
            return (jnp.asarray(np.cos(emb)), jnp.asarray(np.sin(emb)))

        def _rotate_half(x):
            h = x.shape[-1] // 2
            return jnp.concatenate([-x[..., h:], x[..., :h]], axis=-1)

        def _rmsnorm(v, w):
            return v * jax.lax.rsqrt(jnp.mean(v * v, axis=-1, keepdims=True) + EPS_RMS) * w
        Bx, Tx, Cx = x.shape
        h = _rmsnorm(x, ln1_w)
        q = (h @ wq.T).reshape(Bx, Tx, NH, HD).transpose(0, 2, 1, 3)
        k = (h @ wk.T).reshape(Bx, Tx, NKV, HD).transpose(0, 2, 1, 3)
        v = (h @ wv.T).reshape(Bx, Tx, NKV, HD).transpose(0, 2, 1, 3)
        cos, sin = _rope_tables(Tx)
        cos, sin = (cos[None, None], sin[None, None])
        q = q * cos + _rotate_half(q) * sin
        k = k * cos + _rotate_half(k) * sin
        k = jnp.repeat(k, NREP, axis=1)
        v = jnp.repeat(v, NREP, axis=1)
        scores = jnp.einsum('bhtd,bhsd->bhts', q, k) / jnp.sqrt(jnp.float32(HD))
        causal = jnp.tril(jnp.ones((Tx, Tx), dtype=bool))
        scores = jnp.where(causal[None, None], scores, jnp.float32(-1e+30))
        att = jax.nn.softmax(scores, axis=-1)
        y = jnp.einsum('bhts,bhsd->bhtd', att, v).transpose(0, 2, 1, 3).reshape(Bx, Tx, Cx)
        x = x + y @ wo.T
        flat = _rmsnorm(x, ln2_w).reshape(-1, Cx)
        probs = jax.nn.softmax(flat @ router_w.T, axis=-1)
        tp, ti = jax.lax.top_k(probs, TOPK)
        tp = tp / (jnp.sum(tp, axis=-1, keepdims=True) + 1e-09)
        weights = jnp.sum(tp[..., None] * jax.nn.one_hot(ti, NE, dtype=flat.dtype), axis=1)
        out = jnp.zeros_like(flat)
        for e in range(NE):
            hh = jax.nn.silu(flat @ w1[e].T) * (flat @ w3[e].T)
            out = out + weights[:, e:e + 1] * (hh @ w2[e].T)
        return x + out.reshape(Bx, Tx, Cx)

    def _L1_gnn_ref(feat, src, dst, rel, W_rel, b_rel, W_ih, b_ih, b_hh, W1, b1, W2, b2, W3, b3):
        import jax, jax.numpy as jnp
        import numpy as np
        N_NODES = 10000
        N_EDGES = 10000
        D = 256
        D_OUT = 256
        NUM_REL = 2
        n_nodes = feat.shape[0]
        S = feat[src]

        def edge_nn(x, W, b):
            h = jax.nn.relu(x @ W.T + b)
            return jax.nn.relu(h @ W.T + b)
        msgs = jnp.zeros_like(S)
        for r in range(W_rel.shape[0]):
            msgs = jnp.where((rel == r)[:, None], edge_nn(S, W_rel[r], b_rel[r]), msgs)
        agg = jax.ops.segment_sum(msgs, dst, num_segments=n_nodes)
        gates = agg @ W_ih.T + b_ih + b_hh
        i, f, g, o = jnp.split(gates, 4, axis=-1)
        c = jax.nn.sigmoid(i) * jnp.tanh(g)
        hn = jax.nn.sigmoid(o) * jnp.tanh(c)
        x = jax.nn.relu(hn @ W1.T + b1)
        x = jax.nn.relu(x @ W2.T + b2)
        return x @ W3.T + b3

    def _L1_ffn_ref(x, gamma, beta, Wr, br, W1, b1, W2, b2):
        import jax, jax.numpy as jnp
        import numpy as np
        E = 8
        K = 2
        D = 256
        H = 512
        DOUT = 256
        EPS = 1e-05
        mu = jnp.mean(x, axis=-1, keepdims=True)
        var = jnp.mean(jnp.square(x - mu), axis=-1, keepdims=True)
        xn = (x - mu) * jax.lax.rsqrt(var + EPS) * gamma + beta
        logits = jnp.einsum('bsd,de->bse', xn, Wr) + br
        top_vals, top_idx = jax.lax.top_k(logits, K)
        w = jax.nn.softmax(top_vals, axis=-1)
        w_full = jnp.einsum('bsk,bske->bse', w, jax.nn.one_hot(top_idx, E, dtype=w.dtype))
        y = jnp.zeros(x.shape[:-1] + (DOUT,), x.dtype)
        for e in range(E):
            h = jax.nn.gelu(jnp.einsum('bsd,dh->bsh', xn, W1[e]) + b1[e], approximate=False)
            y_e = jnp.einsum('bsh,hd->bsd', h, W2[e]) + b2[e]
            y = y + y_e * w_full[..., e, None]
        return y

    def _L2_gnn_ref(x, W_u, b_u, W_v, src, dst):
        import jax, jax.numpy as jnp
        import numpy as np
        N_NODES = 50000
        N_EDGES = 25000
        DIM = 256
        NUM_HEADS = 8
        n_nodes, dim = x.shape
        num_heads = W_u.shape[0]
        head_dim = dim // num_heads
        s_u = x @ W_u.T + b_u
        s_v = x @ W_v.T
        e = s_u[src] + s_v[dst]
        e = jnp.where(e >= 0, e, 0.2 * e)
        m = jax.ops.segment_max(e, dst, num_segments=n_nodes)
        e_exp = jnp.exp(e - m[dst])
        denom = jax.ops.segment_sum(e_exp, dst, num_segments=n_nodes)
        probs = e_exp / denom[dst]
        xh = x.reshape(n_nodes, head_dim, num_heads)
        msg = xh[src] * probs[:, None, :]
        out = jax.ops.segment_sum(msg, dst, num_segments=n_nodes)
        return out.reshape(n_nodes, dim)

    def _L2_ffn_ref(input_embeddings, router_w, w1, b1, w2, b2):
        import jax, jax.numpy as jnp
        import numpy as np
        NUM_EXPERTS = 8
        TOP_K = 2
        B, S, D = (8, 256, 256)

        def _moe(tokens, router_w, w1, b1, w2, b2):
            N = tokens.shape[0]
            E = router_w.shape[0]
            logits = tokens.astype(jnp.float32) @ router_w.astype(jnp.float32).T
            probs = jax.nn.softmax(logits, axis=-1)
            rw, re = jax.lax.top_k(probs, TOP_K)
            if TOP_K > 1:
                rw = rw / jnp.maximum(rw.sum(-1, keepdims=True), 1e-12)
            rw = rw.astype(tokens.dtype)
            combine = jnp.zeros((N, E), tokens.dtype).at[jnp.arange(N)[:, None], re].set(rw)
            out = tokens
            for e in range(E):
                h = jax.nn.gelu(tokens @ w1[e] + b1[e], approximate=False)
                y = h @ w2[e] + b2[e]
                out = out + combine[:, e:e + 1] * y
            return out
        b, s, d = input_embeddings.shape
        tokens = input_embeddings.reshape(b * s, d)
        return _moe(tokens, router_w, w1, b1, w2, b2).reshape(b, s, d)

    def _L3_gnn_ref(x, edge_index, dWl1, dWr1, db1, dWl2, dWr2, db2, pool_w, uWl1, uWr1, ub1, uWl2, uWr2, ub2):
        import jax, jax.numpy as jnp
        import numpy as np
        import math
        HIDDEN = 256
        DEPTH = 3
        RATIOS = (0.5, 0.5, 0.5)
        N = 625
        E = 10000

        def _sage_layer(x_src, x_dst, src, dst, emask, Wl, Wr, b):
            n_dst = x_dst.shape[0]
            msgs = x_src[src] * emask[:, None]
            s = jax.ops.segment_sum(msgs, dst, num_segments=n_dst)
            c = jax.ops.segment_sum(emask, dst, num_segments=n_dst)
            agg = s / jnp.maximum(c, 1.0)[:, None]
            return agg @ Wl.T + x_dst @ Wr.T + b

        def _cummean_pad(x_small, n_dst):
            n, d = x_small.shape
            cm = jnp.cumsum(x_small, axis=0) / jnp.arange(1, n + 1, dtype=x_small.dtype)[:, None]
            return jnp.concatenate([cm, jnp.zeros((n_dst - n, d), x_small.dtype)], axis=0)

        def _forward(x, edge_index, dWl1, dWr1, db1, dWl2, dWr2, db2, pool_w, uWl1, uWr1, ub1, uWl2, uWr2, ub2):
            src, dst = (edge_index[0], edge_index[1])
            emask = jnp.ones((src.shape[0],), x.dtype)
            xs = []
            n = x.shape[0]
            for i in range(DEPTH):
                xs.append(x)
                h = jax.nn.relu(_sage_layer(x, x, src, dst, emask, dWl1[i], dWr1[i], db1[i]))
                x = _sage_layer(h, h, src, dst, emask, dWl2[i], dWr2[i], db2[i])
                w_ = pool_w[i]
                score = jnp.tanh(x @ w_ / jnp.linalg.norm(w_))
                k = int(math.ceil(RATIOS[i] * n))
                vals, perm = jax.lax.top_k(score, k)
                x = x[perm] * vals[:, None]
                new_id = jnp.full((n,), -1, jnp.int32).at[perm].set(jnp.arange(k, dtype=jnp.int32))
                s2, d2 = (new_id[src], new_id[dst])
                emask = emask * (s2 >= 0).astype(x.dtype) * (d2 >= 0).astype(x.dtype)
                src, dst = (jnp.maximum(s2, 0), jnp.maximum(d2, 0))
                n = k
            for i in range(DEPTH - 2, -1, -1):
                skip = xs[i]
                n_src, n_dst = (x.shape[0], skip.shape[0])
                agg1 = _cummean_pad(x, n_dst)
                h = jax.nn.relu(agg1 @ uWl1[i].T + skip @ uWr1[i].T + ub1[i])
                agg2 = _cummean_pad(h[:n_src], n_dst)
                x = agg2 @ uWl2[i].T + h @ uWr2[i].T + ub2[i]
            return x
        return _forward(x, edge_index, dWl1, dWr1, db1, dWl2, dWr2, db2, pool_w, uWl1, uWr1, ub1, uWl2, uWr2, ub2)

    def _L3_ffn_ref(x, W1, b1, Wg, bg, Wd, bd):
        import jax, jax.numpy as jnp
        import numpy as np
        C = 256
        HID = 1024
        E = 8
        TEMP = 1.0
        orig_shape = x.shape
        xf = x.reshape(-1, orig_shape[-1])
        H = jax.nn.gelu(xf @ W1 + b1, approximate=False)
        probs = jax.nn.softmax((H @ Wg + bg) / TEMP, axis=-1)
        assign = jnp.argmax(probs, axis=-1)
        out = jnp.zeros_like(xf)
        for e in range(Wd.shape[0]):
            y = H @ Wd[e] + bd[e]
            sel = (assign == e)[:, None]
            out = out + jnp.where(sel, probs[:, e:e + 1] * y, 0.0)
        return out.reshape(orig_shape)
    edge_index = jnp.stack([src, dst])
    x = x + _L0_gnn_ref(_layernorm(x, axis=-1), edge_index, L0_gnn_W_l, L0_gnn_W_r, L0_gnn_b_r)
    x = x + _L0_ffn_ref(_layernorm(x, axis=-1)[None], L0_ffn_ln1_w, L0_ffn_ln2_w, L0_ffn_wq, L0_ffn_wk, L0_ffn_wv, L0_ffn_wo, L0_ffn_router_w, L0_ffn_w1, L0_ffn_w2, L0_ffn_w3)[0]
    x = x + _L1_gnn_ref(_layernorm(x, axis=-1), src, dst, edge_type_2, L1_gnn_W_rel, L1_gnn_b_rel, L1_gnn_W_ih, L1_gnn_b_ih, L1_gnn_b_hh, L1_gnn_W1, L1_gnn_b1, L1_gnn_W2, L1_gnn_b2, L1_gnn_W3, L1_gnn_b3)
    x = x + _L1_ffn_ref(_layernorm(x, axis=-1)[None], L1_ffn_gamma, L1_ffn_beta, L1_ffn_Wr, L1_ffn_br, L1_ffn_W1, L1_ffn_b1, L1_ffn_W2, L1_ffn_b2)[0]
    x = x + _L2_gnn_ref(_layernorm(x, axis=-1), L2_gnn_W_u, L2_gnn_b_u, L2_gnn_W_v, src, dst)
    x = x + _L2_ffn_ref(_layernorm(x, axis=-1)[None], L2_ffn_router_w, L2_ffn_w1, L2_ffn_b1, L2_ffn_w2, L2_ffn_b2)[0]
    x = x + _L3_gnn_ref(_layernorm(x, axis=-1), edge_index, L3_gnn_dWl1, L3_gnn_dWr1, L3_gnn_db1, L3_gnn_dWl2, L3_gnn_dWr2, L3_gnn_db2, L3_gnn_pool_w, L3_gnn_uWl1, L3_gnn_uWr1, L3_gnn_ub1, L3_gnn_uWl2, L3_gnn_uWr2, L3_gnn_ub2)
    x = x + _L3_ffn_ref(_layernorm(x, axis=-1)[None], L3_ffn_W1, L3_ffn_b1, L3_ffn_Wg, L3_ffn_bg, L3_ffn_Wd, L3_ffn_bd)[0]
    return x

_drawn_inputs = setup_inputs


def setup_inputs(seed=0):
    import zlib

    import numpy as np

    out = dict(_drawn_inputs(seed))
    spreads = {'L0_gnn_b_r': (0.0, 0.1),
     'L0_ffn_ln1_w': (1.0, 0.6),
     'L0_ffn_ln2_w': (1.0, 0.6),
     'L1_ffn_br': (0.0, 0.401),
     'L2_ffn_b1': (0.0, 0.56),
     'L2_ffn_b2': (0.0, 0.364),
     'L3_gnn_db1': (0.0, 0.8),
     'L3_gnn_db2': (0.0, 0.8),
     'L3_gnn_ub1': (0.0, 1.0),
     'L3_gnn_ub2': (0.0, 0.526),
     'L3_ffn_b1': (0.0, 0.8),
     'L3_ffn_bg': (0.0, 0.8),
     'L3_ffn_bd': (0.0, 2.0)}
    factors = {'L0_ffn_wq': 8.0,
     'L0_ffn_wk': 8.0,
     'L0_ffn_wv': 4.733,
     'L0_ffn_wo': 4.964,
     'L0_ffn_router_w': 4.881,
     'L0_ffn_w1': 5.132,
     'L0_ffn_w2': 4.229,
     'L0_ffn_w3': 4.682,
     'L1_gnn_b_rel': 3.493,
     'L1_gnn_b_ih': 8.0,
     'L1_gnn_b_hh': 8.0,
     'L1_gnn_b1': 2.707,
     'L1_ffn_gamma': 8.0,
     'L1_ffn_beta': 7.975,
     'L1_ffn_b1': 8.0,
     'L1_ffn_b2': 6.6,
     'L2_gnn_b_u': 8.0,
     'L3_gnn_dWr1': 5.511,
     'L3_ffn_W1': 8.0,
     'L3_ffn_Wg': 8.0,
     'L3_ffn_Wd': 8.0}
    for name, (base, spread) in spreads.items():
        noise = np.random.default_rng([zlib.crc32(name.encode()), seed]).standard_normal(out[name].shape)
        drawn = base * np.exp(spread * noise) if base else spread * noise
        out[name] = jnp.asarray(drawn.astype(out[name].dtype))
    for name, factor in factors.items():
        out[name] = (out[name] * factor).astype(out[name].dtype)
    return out
```

```python
from contextlib import ExitStack

import numpy as np

import concourse.bass as bass
from concourse import mybir

F32 = mybir.dt.float32
BF16 = mybir.dt.bfloat16
F16 = mybir.dt.float16
I32 = mybir.dt.int32
ALU = mybir.AluOpType
ACT = mybir.ActivationFunctionType
AX = mybir.AxisListType

N = 625
D = 256
E = 10000
TP = 125
NT = N // TP
KD = D // 128
NX = 8
HID0 = 682
M0 = -(-HID0 // 128)
ET = E // TP
NG = ET // 2
HALVES = ((0, 375), (375, 250))
HALF_TILES = ((0, 3), (3, 5))
LEVELS = (625, 313, 157, 79)
NEG = -1.0e30
NORMS = 14


def tiles(n):
    return [(t, t * TP, min(TP, n - t * TP)) for t in range(-(-n // TP))]


class Fields:

    def __init__(self, *fields):
        self.at, self.size = {}, 0
        for name, width in fields:
            self.at[name] = (self.size, width)
            self.size += width

    def __call__(self, tensor, name, parts=128):
        a, w = self.at[name]
        return tensor[0:parts, a:a + w]


CONST = Fields(("ident", 128), ("ones", 128), ("iota", 626), ("cos", NT * 64), ("sin", NT * 64),
               ("causal", TP), ("before", TP), ("before8", 64), ("groups", 2 * NG), ("cummean", 3 * 313))
ROWS = Fields(("l0_b_r", D), ("l1_b_rel", 2 * D), ("l1_b3", D), ("l1_br", NX))
ROWS3 = Fields(*[(f"l3_db{k}_{i}", D) for i in range(3) for k in (1, 2)],
              *[(f"l3_ub{k}_{i}", D) for i in range(2) for k in (1, 2)], ("l3_bg", NX))
COLS = Fields(("ln1_w", KD), ("ln2_w", KD), ("b_rel", 2 * KD), ("b_ih", 6), ("b_hh", 6), ("g_b1", 1), ("g_b2", 1),
              ("gamma", KD), ("beta", KD), ("l3_b1", 8), ("b_u", 1))
W0 = Fields(("wl", KD * D), ("wr", KD * D), ("wqkv", KD * 512), ("wo", KD * D), ("router", KD * NX))
W1 = Fields(("w_rel", 2 * KD * D), ("w_ih", KD * 768), ("w1", KD * 128), ("w2", 128), ("w3", D))
WR = Fields(("l1", KD * NX), ("l2", KD * NX), ("l3", 8 * NX), ("wu", KD * NX), ("wv", KD * NX))
WG = Fields(*[(f"d{m}{k}_{i}", KD * D) for i in range(3) for k in (1, 2) for m in "lr"],
            *[(f"u{m}{k}_{i}", KD * D) for i in range(2) for k in (1, 2) for m in "lr"])
SLOT0 = 2 * KD * HID0 + M0 * D


def build(nc, io, out):
    with ExitStack() as ctx:
        def sb(name, shape, dt=F32):
            return ctx.enter_context(nc.sbuf_tensor(name, shape, dt))

        def sem(name):
            return ctx.enter_context(nc.semaphore(name))

        const = sb("const", [128, CONST.size])
        rows = sb("rows", [1, ROWS.size])
        cols = sb("cols", [128, COLS.size])
        w0 = sb("w0", [128, max(W0.size, KD * 1024)])
        w1 = sb("w1", [128, W1.size])
        rows3 = w1[0:1, 0:ROWS3.size]
        wr = sb("wr", [128, WR.size])
        b2s = sb("b2s", [NX, 3 * D])
        poolw = sb("poolw", [TP, 3 * D])
        X = sb("X", [TP, NT, D])
        XN = sb("XN", [TP, NT, D])
        XWE = sb("XWE", [TP, NT, D + 1])
        ROOT = sb("ROOT", [TP, NT, D])
        XT = sb("XT", [128, KD, N])
        ST = sb("ST", [128, KD, N])
        AT = sb("AT", [TP, NT, N])
        MB = sb("MB", [128, NT * N])
        arena = sb("arena", [128, max(2 * NT * N, WG.size)])
        ring = sb("ring", [128, 2, SLOT0])
        HT = sb("HT", [128, 8 * N])
        col = sb("col", [TP, 256])
        gate = sb("gate", [TP, 6, NT, NX])
        comb = sb("comb", [TP, NT, NX])
        combT = sb("combT", [NX, N])
        silu = sb("silu", [128, 2, 375])
        zeros = sb("zeros", [1, 512], BF16)
        bsum = sb("bsum", [128, 6])
        ranges = sb("ranges", [1, 3 * NT], I32)
        inside_ready, ranges_ready = sem("inside_ready"), sem("ranges_ready")
        power = sb("power", [TP, NT])
        scratch = sb("scratch", [TP, 2 * NT * NX * NX])
        power_set, cell_in, tanh_in, tanh_out = (sem(x) for x in ("power_set", "cell_in", "tanh_in", "tanh_out"))

        A0T = arena[0:TP, 0:NT * N].rearrange("p (t n) -> p t n", t=NT)
        A1T = arena[0:TP, NT * N:2 * NT * N].rearrange("p (t n) -> p t n", t=NT)
        AR = (A0T, A1T)
        PS = ctx.enter_context(nc.psum_tensor("PS", [128, 8, 512], F32))
        PF = PS[:, :, :].rearrange("p b n -> p (b n)")

        ident = CONST(const, "ident")
        ones = CONST(const, "ones")

        def wv(tensor, fields, name, k):
            return fields(tensor, name).rearrange("p (k n) -> p k n", k=k)

        const_in, x_in, edges_in, small_in, gnn3_in, w1_3_in = (
            sem(n) for n in ("const_in", "x_in", "edges_in", "small_in", "gnn3_in", "w1_3_in"))
        slot_in = [sem(f"slot_in{b}") for b in range(2)]
        out_done = sem("out_done")
        act_full, act_free = sem("act_full"), sem("act_free")
        dve_full, dve_free = sem("dve_full"), sem("dve_free")
        chain = sem("chain")
        onehots, edge_mm = sem("onehots"), sem("edge_mm")
        adj_full, adj_copied, adj_copied_act = sem("adj_full"), sem("adj_copied"), sem("adj_copied_act")
        var_ready, rstd_ready = sem("var_ready"), sem("rstd_ready")
        xn_ready = sem("xn_ready")
        gnn_weights_used = sem("gnn_weights_used")
        layer_done = sem("layer_done")
        zeros_ready, at_ready, rope_ready = sem("zeros_ready"), sem("at_ready"), sem("rope_ready")
        root_ready = sem("root_ready")
        scores_full, nmax_ready, probs_ready = sem("scores_full"), sem("nmax_ready"), sem("probs_ready")
        pt_full, pt_copied, y_out_full, y_taken = (sem(x) for x in ("pt_full", "pt_copied", "y_out_full", "y_taken"))
        logit_ready, exp_ready, comb_ready = sem("logit_ready"), sem("exp_ready"), sem("comb_ready")
        hid_full, hid_free, y_full, y_used = ({L: sem(f"{x}{L}") for L in range(4)}
                                              for x in ("hid_full", "hid_free", "y_full", "y_used"))
        silu_ready = sem("silu_ready")
        bsum_ready, gates_ready, cell_tanh, cell_ready = (
            sem(x) for x in ("bsum_ready", "gates_ready", "cell_tanh", "cell_ready"))
        uT_ready, v_ready, u_full, raw_done, z02_done, z_done, gat_exp, gat_tr, gat_pt, gat_full, gat_taken = (
            sem(x) for x in ("uT_ready", "v_ready", "u_full", "raw_done", "z02_done", "z_done", "gat_exp", "gat_tr",
                             "gat_pt", "gat_full", "gat_taken"))
        diag_ready, perm_ready, cmt_cleared = sem("diag_ready"), sem("perm_ready"), sem("cmt_cleared")

        def view(tensor, at, parts, *shape):
            size = int(np.prod(shape))
            v = tensor[0:parts, at:at + size]
            if len(shape) == 2:
                v = v.rearrange("p (a b) -> p a b", a=shape[0])
            if len(shape) == 3:
                v = v.rearrange("p (a b c) -> p a b c", a=shape[0], b=shape[1])
            return v

        gate64 = view(scratch, 0, TP, 2, NT, NX * NX)
        nodes = view(MB, 0, TP, 3 * ET).bitcast(I32).rearrange("p (a e) -> p a e", a=3)
        nodef = view(MB, 3 * ET, TP, 3, ET)
        iota16 = view(MB, 6 * ET, TP, 313).bitcast(F16)
        src_hot = HT[0:TP, 0:626].bitcast(BF16).rearrange("p (q n) -> p q n", q=2)
        dst_hot = HT[0:TP, 626:626 + 2 * TP].bitcast(BF16).rearrange("p (q n) -> p q n", q=2)
        inside = view(HT, 1000, TP, NT, ET)
        local = view(HT, 1400, TP, NT, ET)
        work = HT[0:1, 1800:1800 + 3 * NT * NG + 4 * NT]
        qkT = view(HT, 0, 128, 3, N)
        probs = view(HT, 3 * N, TP, 2, N)
        pT = view(HT, 5 * N, TP, 2, NT, TP)
        qk = view(MB, 0, TP, NT, 384)
        vv = view(MB, NT * 384, TP, NT, 128)
        rope = view(ROOT[:, :, :].rearrange("p t n -> p (t n)"), 0, TP, 2, 384)
        attn = XWE
        msg = (XWE, ROOT)
        lstm = view(HT, 0, 128, 6, N)
        uT = combT
        XH = view(HT, 0, TP, NT, NX * 33)
        ex = view(HT, NT * NX * 33, TP, 2, N)
        raw = [view(ring[:, b, :], 1100, TP, NT, N) for b in range(2)]
        zz = ST
        vcol = gate[:, 0]
        maskb = view(MB, 0, TP, NT, N)
        XL = {1: view(MB, 0, TP, 3, D), 2: view(MB, 768, TP, 2, D), 3: view(MB, 1280, TP, 1, D)}
        XLT = {1: view(MB, 1536, 128, KD, 313), 2: view(MB, 2162, 128, KD, 157)}
        PT = view(HT, 0, TP, NT, 313)
        BM = view(HT, NT * 313, TP, NT, 313)
        ADJ = {1: view(HT, 2 * NT * 313, TP, 3, 313), 2: view(HT, (2 * NT + 3) * 313, TP, 2, 157)}
        silu_flat = silu[:, :, :].rearrange("p a n -> p (a n)")
        diag = view(silu_flat, 0, TP, NT, TP)
        CMT = view(silu_flat, 0, 128, KD, 375)
        ST2 = view(MB, 0, 128, KD, N)
        scoreb = scratch[:, 0:N]
        v02 = gate[:, 1]
        xt_of = {1: XT, 2: XT}
        slot_base = {0: 0, 1: 64, 2: 128, 3: 192}

        block = ctx.enter_context(nc.Block())

        @block.tensor
        def _(pe):
            n = {"a": 0, "v": 0, "xn": 0}

            def act_bank():
                if n["a"] >= 4:
                    pe.wait_ge(act_free, n["a"] - 3)
                n["a"] += 1
                return (n["a"] - 1) % 4

            def dve_bank():
                if n["v"] >= 4:
                    pe.wait_ge(dve_free, n["v"] - 3)
                n["v"] += 1
                return 4 + (n["v"] - 1) % 4

            def emptied():
                pe.wait_ge(act_free, n["a"])
                pe.wait_ge(dve_free, n["v"])

            def transposes(src, rows_=N, wait=True):
                ts = tiles(rows_)
                if wait:
                    n["xn"] += len(ts)
                    pe.wait_ge(xn_ready, n["xn"])
                for k in range(KD):
                    for part in (ts[:4], ts[4:]):
                        if not part:
                            continue
                        bank = act_bank() if k else dve_bank()
                        for t, c0, c in part:
                            mm = pe.transpose(PS[:, bank, c0 - part[0][1]:c0 - part[0][1] + c],
                                              src[0:c, t, k * 128:(k + 1) * 128], ident[0:c, 0:c])
                        mm.then_inc(act_full if k else dve_full, 1)

            def row(name):
                return ROWS(rows, name, 1) if name in ROWS.at else ROWS3(rows3, name, 1)

            def bias_row(bank, c, width, name, off=0):
                return pe.matmul(PS[0:c, bank, 0:width], ones[0:1, 0:c], row(name)[:, off:off + width],
                                 start=False, stop=True)

            def sage(src_t, adj, wl, wr_, bias, rows_):
                ts = tiles(rows_)
                for t, c0, c in ts:
                    bank = dve_bank()
                    for k in range(KD):
                        mm = pe.matmul(PS[0:c, bank, 0:D], src_t[:, k, c0:c0 + c], wl[:, k, :],
                                       start=(k == 0), stop=(k == KD - 1))
                    mm.then_inc(dve_full, 1)
                for t, c0, c in ts:
                    bank = act_bank()
                    for k in range(KD):
                        pe.matmul(PS[0:c, bank, 0:D], src_t[:, k, c0:c0 + c], wr_[:, k, :],
                                  start=(k == 0), stop=False)
                    bias_row(bank, c, D, bias).then_inc(act_full, 1)
                pe.wait_ge(dve_free, n["v"])
                for t, c0, c in ts:
                    bank = dve_bank()
                    for s, s0, sc in ts:
                        mm = pe.matmul(PS[0:c, bank, 0:D + 1], adj[0:sc, s, c0:c0 + c], XWE[0:sc, s, :],
                                       start=(s == 0), stop=(s == len(ts) - 1))
                    mm.then_inc(dve_full, 1)

            def logits(src_t, w, kk, bias=None):
                bank = dve_bank()
                for t, c0, c in tiles(N):
                    for k in range(kk):
                        mm = pe.matmul(PS[0:TP, bank, t * NX:(t + 1) * NX], src_t[:, k, c0:c0 + c], w[:, k, :],
                                       start=(k == 0), stop=(k == kk - 1 and bias is None))
                    if bias is not None:
                        mm = pe.matmul(PS[0:TP, bank, t * NX:(t + 1) * NX], ones[0:1, 0:TP], row(bias),
                                       start=False, stop=True)
                mm.then_inc(dve_full, 1)

            def bias2(which):
                pe.wait_ge(comb_ready, which + 1)
                for part in (range(4), range(4, 5)):
                    bank = dve_bank()
                    for t in part:
                        mm = pe.transpose(PS[0:NX, bank, (t - part[0]) * TP:(t - part[0] + 1) * TP],
                                          comb[:, t, :], ident[0:TP, 0:TP])
                    mm.then_inc(dve_full, 1)
                pe.wait_ge(dve_free, n["v"])
                for t in range(NT):
                    bank = dve_bank()
                    pe.matmul(PS[0:TP, bank, 0:D], combT[:, t * TP:(t + 1) * TP], b2s[:, (which - 1) * D:which * D],
                              start=True, stop=True).then_inc(dve_full, 1)

            def y_out(L, i, b, hid, w2, blocks, h_tiles):
                for t in h_tiles:
                    if t % 2 == 0:
                        pe.wait_ge(y_used[L], i * 10 + (5 * b + min(t + 2, NT)))
                    for k in range(blocks):
                        rows_ = min(128, HID0 - k * 128) if L == 0 else 128
                        mm = pe.matmul(PS[0:TP, 5 + t // 2, (t % 2) * D:(t % 2 + 1) * D],
                                       hid[0:rows_, k, t * TP:(t + 1) * TP], w2[0:rows_, k, :],
                                       start=(k == 0), stop=(k == blocks - 1))
                    mm.then_inc(y_full[L], 1)

            def edges():
                pe.wait_ge(const_in, 16)
                pe.wait_ge(inside_ready, NT)
                for d in range(NT):
                    mm = pe.matmul(PS[0:1, 7, d * ET:(d + 1) * ET], ones[0:TP, 0:1], inside[:, d, :],
                                   start=True, stop=True)
                mm.then_inc(dve_full, 4)
                n["v"] = 4
                pe.wait_ge(ranges_ready, 1)
                for d in range(NT):
                    start = pe.value_load(ranges[0:1, d:d + 1], min_val=0, max_val=NG - 1)
                    stop = pe.value_load(ranges[0:1, NT + d:NT + d + 1], min_val=1, max_val=NG)
                    shift = pe.value_load(ranges[0:1, 2 * NT + d:2 * NT + d + 1], min_val=0, max_val=NT * NG)
                    if d:
                        pe.wait_ge(adj_copied, d)
                        pe.wait_ge(adj_copied_act, d)
                    else:
                        pe.wait_ge(zeros_ready, 1)
                    for m in range(NT):
                        pe.matmul(PS[0:TP, m, 0:2 * TP], zeros[:, 0:TP], zeros[:, 0:2 * TP], start=True, stop=False)
                    with pe.Fori(start, stop) as i:
                        for q in range(2):
                            pe.wait_ge(onehots, shift * 2 + i * 2 + (q + 1))
                            for m in range(NT):
                                mm = pe.matmul(PS[0:TP, m, 0:2 * TP], src_hot[:, q, m * TP:(m + 1) * TP],
                                               dst_hot[:, q, :], start=False, stop=False)
                            mm.then_inc(edge_mm, 1)
                    for m in range(NT):
                        mm = pe.matmul(PS[0:TP, m, 0:2 * TP], zeros[:, 0:TP], zeros[:, 0:2 * TP],
                                       start=False, stop=True)
                    mm.then_inc(adj_full, 1)
                pe.wait_ge(adj_copied, NT)
                pe.wait_ge(adj_copied_act, NT)

            def layer0_gnn():
                pe.wait_ge(small_in, 16 * 7)
                transposes(XN)
                emptied()
                pe.wait_ge(at_ready, 1)
                sage(XT, AT, wv(w0, W0, "wl", KD), wv(w0, W0, "wr", KD), "l0_b_r", N)

            def layer0_attention():
                transposes(ROOT)
                emptied()
                wqkv = wv(w0, W0, "wqkv", KD)
                for t, c0, c in tiles(N):
                    bank = dve_bank()
                    for k in range(KD):
                        mm = pe.matmul(PS[0:c, bank, :], XT[:, k, c0:c0 + c], wqkv[:, k, :],
                                       start=(k == 0), stop=(k == KD - 1))
                    mm.then_inc(dve_full, 1)
                for t, c0, c in tiles(N):
                    pe.wait_ge(rope_ready, t + 1)
                    bank = dve_bank()
                    for k in range(3):
                        mm = pe.transpose(PS[:, bank, k * TP:(k + 1) * TP], qk[:, t, k * 128:(k + 1) * 128],
                                          ident[0:TP, 0:TP])
                    mm.then_inc(dve_full, 1)
                emptied()
                steps = [(h, t) for h in range(4) for t in range(NT)]

                def scores(n_):
                    h, t = steps[n_]
                    p0, blk, base, keys = 64 * (h // 2), h % 2, (n_ % 2) * 2, (t + 1) * TP
                    if n_ >= 2:
                        pe.wait_ge(probs_ready, n_ - 1)
                    for c0, c1 in ((0, min(keys, 512)), (512, keys)):
                        if c1 <= c0:
                            continue
                        diag_ = c1 > t * TP
                        pe.matmul(PF[0:TP, base * 512 + c0:base * 512 + c1],
                                  qkT[p0:p0 + 64, blk, t * TP:(t + 1) * TP], qkT[p0:p0 + 64, 2, c0:c1],
                                  start=True, stop=not diag_)
                        if diag_:
                            d0 = max(t * TP, c0)
                            mm = pe.matmul(PF[0:TP, base * 512 + d0:base * 512 + c1], ident[0:TP, 0:TP],
                                           CONST(const, "causal", TP)[:, d0 - t * TP:c1 - t * TP],
                                           start=False, stop=True)
                    mm.then_inc(scores_full, 1)

                def turn(n_):
                    h, t = steps[n_]
                    q, pt = n_ % 2, 4 + 2 * (n_ % 2)
                    pe.wait_ge(probs_ready, n_ + 1)
                    if n_ >= 2:
                        pe.wait_ge(pt_copied, n_ - 1)
                        pe.wait_ge(y_taken, n_ - 1)
                    for kb in range(t + 1):
                        at = pt * 512 + kb * 128
                        mm = pe.transpose(PF[0:TP, at:at + TP], probs[:, q, kb * TP:(kb + 1) * TP],
                                          ident[0:TP, 0:TP])
                    mm.then_inc(pt_full, 1)

                def output(n_):
                    h, t = steps[n_]
                    q, pt = n_ % 2, 4 + 2 * (n_ % 2)
                    pe.wait_ge(pt_copied, n_ + 1)
                    for kb in range(t + 1):
                        mm = pe.matmul(PS[0:TP, pt + 1, 256:320], pT[:, q, kb, :],
                                       vv[:, kb, (h // 2) * 64:(h // 2 + 1) * 64],
                                       start=(kb == 0), stop=(kb == t))
                    mm.then_inc(y_out_full, 1)

                scores(0)
                for n_ in range(len(steps) + 1):
                    if n_ + 1 < len(steps):
                        scores(n_ + 1)
                    if n_ < len(steps):
                        turn(n_)
                    if n_ >= 1:
                        output(n_ - 1)
                pe.wait_ge(y_taken, len(steps))
                transposes(attn, wait=False)
                emptied()
                wo = wv(w0, W0, "wo", KD)
                for t, c0, c in tiles(N):
                    bank = dve_bank()
                    for k in range(KD):
                        mm = pe.matmul(PS[0:c, bank, 0:D], XT[:, k, c0:c0 + c], wo[:, k, :],
                                       start=(k == 0), stop=(k == KD - 1))
                    mm.then_inc(dve_full, 1)

            def layer0_moe():
                transposes(ROOT)
                emptied()
                logits(XT, wv(w0, W0, "router", KD), KD)
                pe.wait_ge(dve_free, n["v"])
                hid = HT[:, 0:M0 * N].rearrange("p (m n) -> p m n", m=M0)
                with pe.Fori(0, NX // 2) as i:
                    for b in range(2):
                        slot = ring[:, b, :]
                        w1_ = slot[:, 0:KD * HID0].rearrange("p (k n) -> p k n", k=KD)
                        w3_ = slot[:, KD * HID0:2 * KD * HID0].rearrange("p (k n) -> p k n", k=KD)
                        w2_ = slot[:, 2 * KD * HID0:SLOT0].rearrange("p (k n) -> p k n", k=M0)
                        pe.wait_ge(slot_in[b], i * 16 + 16)
                        for half, (c0, c) in enumerate(HALVES):
                            for m in range(M0):
                                mw = min(128, HID0 - m * 128)
                                ch = (b * 2 + half) * M0 + m
                                pe.wait_ge(hid_free[0], i * 24 + (ch + 1))
                                for j, w in enumerate((w1_, w3_)):
                                    for k in range(KD):
                                        mm = pe.matmul(PS[0:mw, (ch % 2) * 2 + j, 0:c],
                                                       w[:, k, m * 128:m * 128 + mw], XT[:, k, c0:c0 + c],
                                                       start=(k == 0), stop=(k == KD - 1))
                                mm.then_inc(hid_full[0], 1)
                            if half:
                                y_out(0, i, b, hid, w2_, M0, range(*HALF_TILES[0]))
                                pe.wait_ge(hid_free[0], i * 24 + (2 + (b * 2 + 2) * M0))
                                y_out(0, i, b, hid, w2_, M0, range(*HALF_TILES[1]))

            def moe(L, blocks, floats1):
                hid = HT[:, 0:blocks * N].rearrange("p (m n) -> p m n", m=blocks)
                per = 2 * blocks
                with pe.Fori(0, NX // 2) as i:
                    for b in range(2):
                        w1_ = ring[:, b, 0:floats1].rearrange("p (k n) -> p k n", k=KD)
                        w2_ = ring[:, b, floats1:floats1 + blocks * D].rearrange("p (k n) -> p k n", k=blocks)
                        pe.wait_ge(slot_in[b], i * 16 + (16 + slot_base[L]))
                        for half, (c0, c) in enumerate(HALVES):
                            for m in range(blocks):
                                ch = (b * 2 + half) * blocks + m
                                pe.wait_ge(hid_free[L], i * (2 * per) + (ch + 1))
                                for k in range(KD):
                                    mm = pe.matmul(PS[:, ch % 4, 0:c], w1_[:, k, m * 128:(m + 1) * 128],
                                                   xt_of[L][:, k, c0:c0 + c], start=(k == 0), stop=(k == KD - 1))
                                mm.then_inc(hid_full[L], 1)
                        pe.wait_ge(hid_free[L], i * (2 * per) + (4 + (b * 2 + 1) * blocks))
                        y_out(L, i, b, hid, w2_, blocks, range(*HALF_TILES[0]))
                        pe.wait_ge(hid_free[L], i * (2 * per) + (4 + (b * 2 + 2) * blocks))
                        y_out(L, i, b, hid, w2_, blocks, range(*HALF_TILES[1]))

            def feature_major(w, kk, m_blocks, src, m0=0):
                for m in range(m0, m0 + m_blocks):
                    for c0, c in HALVES:
                        bank = act_bank()
                        for k in range(kk):
                            mm = pe.matmul(PS[:, bank, 0:c], w[:, k, m * 128:(m + 1) * 128], src[:, k, c0:c0 + c],
                                           start=(k == 0), stop=(k == kk - 1))
                        mm.then_inc(act_full, 1)

            def layer1_gnn():
                transposes(XN)
                emptied()
                w_rel = W1(w1, "w_rel").rearrange("p (r k n) -> p r k n", r=2, k=KD)
                for r in range(2):
                    feature_major(w_rel[:, r], KD, KD, XT)
                    pe.wait_ge(act_free, n["a"])
                    for t, c0, c in tiles(N):
                        bank = dve_bank()
                        for k in range(KD):
                            pe.matmul(PS[0:c, bank, 0:D], ST[:, k, c0:c0 + c], w_rel[:, r, k, :],
                                      start=(k == 0), stop=False)
                        bias_row(bank, c, D, "l1_b_rel", off=r * D).then_inc(dve_full, 1)
                    pe.wait_ge(dve_free, n["v"])
                for m in range(KD):
                    for c0, c in HALVES:
                        bank = act_bank()
                        for r in range(2):
                            for s in range(NT):
                                mm = pe.matmul(PS[:, bank, 0:c], msg[r][:, s, m * 128:(m + 1) * 128],
                                               AR[r][:, s, c0:c0 + c], start=(r == 0 and s == 0),
                                               stop=(r == 1 and s == NT - 1))
                        mm.then_inc(act_full, 1)
                pe.wait_ge(act_free, n["a"])
                pe.sem_inc(gnn_weights_used, 1)
                feature_major(wv(w1, W1, "w_ih", KD), KD, 6, ST)
                pe.wait_ge(cell_ready, 2)
                feature_major(wv(w1, W1, "w1", KD), KD, 1, XT)
                pe.wait_ge(act_free, n["a"])
                feature_major(wv(w1, W1, "w2", 1), 1, 1, ST[:, 0:1, :])
                pe.wait_ge(act_free, n["a"])
                for t, c0, c in tiles(N):
                    bank = dve_bank()
                    pe.matmul(PS[0:c, bank, 0:D], ST[:, 1, c0:c0 + c], W1(w1, "w3"), start=True, stop=False)
                    bias_row(bank, c, D, "l1_b3").then_inc(dve_full, 1)
                emptied()
                pe.sem_inc(gnn_weights_used, 1)

            def layer1_moe():
                transposes(ROOT)
                emptied()
                logits(XT, wv(wr, WR, "l1", KD), KD, "l1_br")
                bias2(1)
                pe.wait_ge(dve_free, n["v"])
                moe(1, 4, KD * 512)

            def layer2_gnn():
                transposes(XN)
                emptied()
                for c0, c in HALVES:
                    bank = act_bank()
                    for k in range(KD):
                        mm = pe.matmul(PS[0:NX, bank, 0:c], wv(wr, WR, "wu", KD)[:, k, :], XT[:, k, c0:c0 + c],
                                       start=(k == 0), stop=(k == KD - 1))
                    mm.then_inc(act_full, 1)
                logits(XT, wv(wr, WR, "wv", KD), KD)
                for d in range(NT):
                    for part in (range(4), range(4, 5)):
                        bank = dve_bank()
                        for s in part:
                            mm = pe.transpose(PS[0:TP, bank, (s - part[0]) * TP:(s - part[0] + 1) * TP],
                                              AT[:, s, d * TP:(d + 1) * TP], ident[0:TP, 0:TP])
                        mm.then_inc(dve_full, 1)
                emptied()
                steps = NX * NT

                def u_rows(h):
                    if h:
                        pe.wait_ge(raw_done, h * NT)
                    for c0, c1 in ((0, 512), (512, N)):
                        mm = pe.matmul(PF[0:TP, c0:c1],
                                       ident[0:NX, h:h + 1].broadcast_to([NX, TP]), uT[:, c0:c1],
                                       start=True, stop=True)
                    mm.then_inc(u_full, 1)

                def turn(n_):
                    q, pt = n_ % 2, 4 + 2 * (n_ % 2)
                    pe.wait_ge(gat_exp, n_ + 1)
                    if n_ >= 2:
                        pe.wait_ge(gat_pt, n_ - 1)
                    for s in range(NT):
                        at = pt * 512 + s * 128
                        mm = pe.transpose(PF[0:TP, at:at + TP], ex[:, q, s * TP:(s + 1) * TP], ident[0:TP, 0:TP])
                    mm.then_inc(gat_tr, 1)

                def output(n_):
                    h, t = divmod(n_, NT)
                    pe.wait_ge(gat_pt, n_ + 1)
                    if t == 0 and h >= 2:
                        pe.wait_ge(gat_taken, h - 1)
                    for s in range(NT):
                        mm = pe.matmul(PS[0:TP, 2 + h % 2, 33 * t:33 * t + 33], pT[:, n_ % 2, s, :],
                                       XH[:, s, h * 33:(h + 1) * 33], start=(s == 0), stop=(s == NT - 1))
                    mm.then_inc(gat_full, 1)

                u_rows(0)
                for n_ in range(steps + 1):
                    if n_ >= 1:
                        output(n_ - 1)
                    if n_ % NT == 0 and n_ // NT + 1 < NX:
                        u_rows(n_ // NT + 1)
                    if n_ < steps:
                        turn(n_)

            def layer2_moe():
                transposes(XN)
                emptied()
                logits(XT, wv(wr, WR, "l2", KD), KD)
                bias2(2)
                pe.wait_ge(dve_free, n["v"])
                moe(2, 2, KD * D)

            def gw(name):
                return wv(arena, WG, name, KD)

            def layer3_gnn():
                pe.wait_ge(gnn3_in, 32)
                for i in range(3):
                    rows_, kept = LEVELS[i], LEVELS[i + 1]
                    ts, ks = tiles(rows_), tiles(kept)
                    xin, xt = (XN, XT) if i == 0 else (XL[i], XLT[i])
                    adj = AT if i == 0 else ADJ[i]
                    transposes(xin, rows_)
                    emptied()
                    sage(xt, adj, gw(f"dl1_{i}"), gw(f"dr1_{i}"), f"l3_db1_{i}", rows_)
                    transposes(ROOT, rows_)
                    emptied()
                    sage(ST, adj, gw(f"dl2_{i}"), gw(f"dr2_{i}"), f"l3_db2_{i}", rows_)
                    pe.wait_ge(diag_ready, i + 1)
                    emptied()
                    for part in (ts[:4], ts[4:]):
                        if not part:
                            continue
                        bank = dve_bank()
                        for t, c0, c in part:
                            mm = pe.matmul(PS[0:TP, bank, c0 - part[0][1]:c0 - part[0][1] + c],
                                           ones[0:c, 0:TP], diag[0:c, t, 0:c], start=True, stop=True)
                        mm.then_inc(dve_full, 1)
                    pe.wait_ge(perm_ready, i + 1)
                    for kt, k0, kc in ks:
                        bank = dve_bank()
                        for t, c0, c in ts:
                            mm = pe.matmul(PS[0:kc, bank, 0:D], PT[0:c, t, k0:k0 + kc], ROOT[0:c, t, :],
                                           start=(t == 0), stop=(t == len(ts) - 1))
                        mm.then_inc(dve_full, 1)
                    if i < 2:
                        for t, c0, c in ts:
                            bank = act_bank()
                            for s, s0, sc in ts:
                                mm = pe.matmul(PS[0:c, bank, 0:kept], adj[0:sc, s, c0:c0 + c], PT[0:sc, s, 0:kept],
                                               start=(s == 0), stop=(s == len(ts) - 1))
                            mm.then_inc(act_full, 1)
                        pe.wait_ge(act_free, n["a"])
                        for kt, k0, kc in ks:
                            bank = act_bank()
                            for t, c0, c in ts:
                                mm = pe.matmul(PS[0:kc, bank, 0:kept], BM[0:c, t, k0:k0 + kc], PT[0:c, t, 0:kept],
                                               start=(t == 0), stop=(t == len(ts) - 1))
                            mm.then_inc(act_full, 1)
                emptied()
                cm = CONST(const, "cummean", TP).rearrange("p (t n) -> p t n", t=3)
                src, small = XL[3], LEVELS[3]
                for i in (1, 0):
                    rows_, skip_t = LEVELS[i], (XT if i == 0 else XLT[1])
                    ss, ts = tiles(small), tiles(rows_)

                    def running_mean(src_, rows_src):
                        for k in range(KD):
                            bank = act_bank()
                            for t, c0, c in tiles(rows_src):
                                mm = pe.matmul(PS[:, bank, 0:rows_src], src_[0:c, t, k * 128:(k + 1) * 128],
                                               cm[0:c, t, 0:rows_src], start=(t == 0),
                                               stop=(t == len(tiles(rows_src)) - 1))
                            mm.then_inc(act_full, 1)
                        emptied()

                    def combine(wl, wr_, bias, other):
                        for t, c0, c in ts:
                            bank = dve_bank()
                            for k in range(KD):
                                pe.matmul(PS[0:c, bank, 0:D], other[:, k, c0:c0 + c], wr_[:, k, :],
                                          start=(k == 0), stop=False)
                            if c0 < small:
                                for k in range(KD):
                                    pe.matmul(PS[0:c, bank, 0:D], CMT[:, k, c0:c0 + c], wl[:, k, :],
                                              start=False, stop=False)
                            bias_row(bank, c, D, bias).then_inc(dve_full, 1)

                    pe.wait_ge(cmt_cleared, 1)
                    running_mean(src, small)
                    combine(gw(f"ul1_{i}"), gw(f"ur1_{i}"), f"l3_ub1_{i}", skip_t)
                    emptied()
                    transposes(ROOT, rows_, wait=False)
                    running_mean(ROOT, small)
                    combine(gw(f"ul2_{i}"), gw(f"ur2_{i}"), f"l3_ub2_{i}", ST)
                    emptied()
                    src, small = XN, rows_

            def layer3_moe():
                transposes(XN)
                emptied()
                pe.wait_ge(w1_3_in, 16)
                w1_3 = w0[:, 0:KD * 1024].rearrange("p (k n) -> p k n", k=KD)
                feature_major(w1_3, KD, 8, XT)
                emptied()
                hid = HT[:, :].rearrange("p (m n) -> p m n", m=8)
                logits(hid, wv(wr, WR, "l3", 8), 8, "l3_bg")
                bias2(3)
                pe.wait_ge(dve_free, n["v"])
                with pe.Fori(0, NX // 2) as i:
                    for b in range(2):
                        wd = ring[:, b, 0:8 * D].rearrange("p (k n) -> p k n", k=8)
                        pe.wait_ge(slot_in[b], i * 16 + (16 + slot_base[3]))
                        y_out(3, i, b, hid, wd, 8, range(NT))

            pe.sem_inc(edge_mm, 2 * NG + 2)
            edges()
            layer0_gnn()
            layer0_attention()
            layer0_moe()
            layer1_gnn()
            layer1_moe()
            layer2_gnn()
            layer2_moe()
            layer3_gnn()
            layer3_moe()

        @block.vector
        def _(dve):
            n = {"v": 0, "chain": 0, "root": 0, "norm": 0}

            def link(ins):
                n["chain"] += 1
                ins.then_inc(chain, 1)
                dve.wait_ge(chain, n["chain"])

            def taken(ins):
                ins.then_inc(dve_free, 1)

            def bank():
                n["v"] += 1
                dve.wait_ge(dve_full, n["v"])
                return 4 + (n["v"] - 1) % 4

            def own_banks():
                dve.wait_ge(dve_free, n["v"])

            def rstd(power_base):
                n["norm"] += 1
                power_base.then_inc(var_ready, 1)
                dve.wait_ge(rstd_ready, n["norm"])

            def turned(pt):
                return PF[0:TP, pt * 512:pt * 512 + NT * 128].rearrange("p (k n) -> p k n", k=NT)[:, :, 0:TP]

            def layer_norm(src, dst, signal):
                stats = col[:, 32:32 + NT * 6].rearrange("p (t s) -> p t s", t=NT)
                mv = col[:, 64:64 + NT * 2].rearrange("p (t s) -> p t s", t=NT)
                for t in range(NT):
                    ins = dve.bn_stats(stats[:, t, :], src[:, t, 0:D])
                link(ins)
                for t in range(NT):
                    ins = dve.bn_aggr(mv[:, t, :], stats[:, t, :])
                link(ins)
                rstd(dve.tensor_scalar(col[:, 0:NT], mv[:, :, 1], 1e-5, None, ALU.add))
                for t in range(NT):
                    ins = dve.tensor_scalar(dst[:, t, 0:D], src[:, t, 0:D], mv[:, t, 0:1], col[:, 8 + t:9 + t],
                                            ALU.subtract, ALU.mult)
                    if signal:
                        ins.then_inc(xn_ready, 1)
                if not signal:
                    link(dve.tensor_copy(col[:, 16:17], col[:, 0:1]))

            def rms_norm():
                for t in range(NT):
                    ins = dve.tensor_tensor_reduce(ROOT[:, t, :], XN[:, t, :], XN[:, t, :], 1.0, 0.0, ALU.mult,
                                                   ALU.add, col[:, 24 + t:25 + t])
                link(ins)
                rstd(dve.tensor_scalar(col[:, 0:NT], col[:, 24:24 + NT], 1.0 / D, 1e-6, ALU.mult, ALU.add))
                for t in range(NT):
                    dve.tensor_scalar(ROOT[:, t, :], XN[:, t, :], col[:, 8 + t:9 + t], None,
                                      ALU.mult).then_inc(xn_ready, 1)

            def take_transposes(dst, rows_=N, scale=None, bias=None):
                ts = tiles(rows_)
                for part in (ts[:4], ts[4:]):
                    if not part:
                        continue
                    c0, c1 = part[0][1], part[-1][1] + part[-1][2]
                    b = bank()
                    if scale is None:
                        taken(dve.tensor_copy(dst[:, 0, c0:c1], PS[:, b, 0:c1 - c0]))
                    elif bias is None:
                        taken(dve.tensor_scalar(dst[:, 0, c0:c1], PS[:, b, 0:c1 - c0], scale[:, 0:1], None, ALU.mult))
                    else:
                        taken(dve.tensor_scalar(dst[:, 0, c0:c1], PS[:, b, 0:c1 - c0], scale[:, 0:1], bias[:, 0:1],
                                                ALU.mult, ALU.add))

            def sage(rows_, level, first, finish):
                ts = tiles(rows_)
                for t, c0, c in ts:
                    b = bank()
                    taken(dve.tensor_copy(XWE[0:c, t, 0:D], PS[0:c, b, 0:D]))
                rd = 80 + 8 * level
                for t, c0, c in ts:
                    n["root"] += 1
                    b = bank()
                    if first:
                        link(dve.tensor_scalar(col[0:c, 120 + t:121 + t], PS[0:c, b, D:D + 1], 1.0, None, ALU.max))
                        link(dve.reciprocal(col[0:c, rd + t:rd + t + 1], col[0:c, 120 + t:121 + t]))
                    dve.wait_ge(root_ready, n["root"])
                    ins = dve.scalar_tensor_tensor(ROOT[0:c, t, :], PS[0:c, b, 0:D], col[0:c, rd + t:rd + t + 1],
                                                   ROOT[0:c, t, :], ALU.mult, ALU.add)
                    taken(ins)
                    own_banks()
                    finish(t, c)

            def add_to_x(t, c):
                dve.tensor_tensor(X[0:c, t, :], X[0:c, t, :], ROOT[0:c, t, :], ALU.add).then_inc(chain, 1)
                n["chain"] += 1

            def chained():
                dve.wait_ge(chain, n["chain"])

            def relu_root(t, c):
                dve.tensor_scalar(ROOT[0:c, t, :], ROOT[0:c, t, :], 0.0, None, ALU.max).then_inc(xn_ready, 1)

            def gating(L):
                lg, ev, pr, key, rank, sel = (gate[:, j] for j in range(6))
                s5 = [col[:, 128 + 8 * j:128 + 8 * j + NT] for j in range(4)]

                def wide(v):
                    return v.unsqueeze(2).broadcast_to([TP, NT, NX])

                b = bank()
                taken(dve.tensor_copy(lg, PS[0:TP, b, 0:NT * NX].rearrange("p (t e) -> p t e", t=NT)))
                own_banks()
                link(dve.tensor_reduce(s5[0], lg, AX.X, ALU.max))
                dve.tensor_tensor(ev, lg, wide(s5[0]), ALU.subtract).then_inc(logit_ready, 1)
                dve.wait_ge(exp_ready, L + 1)
                link(dve.tensor_reduce(s5[1], ev, AX.X, ALU.add))
                link(dve.reciprocal(s5[2], s5[1]))
                link(dve.tensor_tensor(pr, ev, wide(s5[2]), ALU.mult))
                k = lg if L == 1 else pr
                greater = gate64[:, 0].rearrange("p t (e j) -> p t e j", e=NX)
                equal = gate64[:, 1].rearrange("p t (e j) -> p t e j", e=NX)
                other = k.unsqueeze(2).broadcast_to([TP, NT, NX, NX])
                own = k.unsqueeze(3).broadcast_to([TP, NT, NX, NX])
                before8 = CONST(const, "before8", TP).unsqueeze(1).broadcast_to([TP, NT, NX * NX])
                dve.tensor_tensor(greater, other, own, ALU.is_gt)
                link(dve.tensor_tensor(equal, other, own, ALU.is_equal))
                link(dve.tensor_tensor(gate64[:, 1], gate64[:, 1], before8, ALU.mult))
                link(dve.tensor_tensor(gate64[:, 0], gate64[:, 0], gate64[:, 1], ALU.add))
                link(dve.tensor_reduce(rank, greater, AX.X, ALU.add))
                top = 0.5 if L == 3 else 1.5
                link(dve.scalar_tensor_tensor(sel, rank, top, ev if L == 1 else pr, ALU.is_lt, ALU.mult))
                if L == 3:
                    link(dve.tensor_copy(comb[:, :, :], sel))
                else:
                    link(dve.tensor_reduce(s5[3], sel, AX.X, ALU.add))
                    if L == 0:
                        link(dve.tensor_scalar(s5[3], s5[3], 1e-9, None, ALU.add))
                    if L == 2:
                        link(dve.tensor_scalar(s5[3], s5[3], 1e-12, None, ALU.max))
                    link(dve.reciprocal(s5[2], s5[3]))
                    link(dve.tensor_tensor(comb[:, :, :], sel, wide(s5[2]), ALU.mult))
                dve.sem_inc(comb_ready, 1)

            def take_bias2():
                for c0, c in ((0, 500), (500, 125)):
                    b = bank()
                    taken(dve.tensor_copy(combT[:, c0:c0 + c], PS[0:NX, b, 0:c]))
                for t in range(NT):
                    b = bank()
                    taken(dve.tensor_tensor(X[:, t, :], X[:, t, :], PS[0:TP, b, 0:D], ALU.add))
                own_banks()

            def add_expert(L, i, b, h_tiles):
                for t in h_tiles:
                    if t % 2 == 0:
                        dve.wait_ge(y_full[L], i * 10 + (5 * b + min(t + 2, NT)))
                    dve.wait_ge(y_used[L], i * 10 + (5 * b + t + 1))
                    dve.scalar_tensor_tensor(X[:, t, :], PS[0:TP, 5 + t // 2, (t % 2) * D:(t % 2 + 1) * D],
                                             comb[:, t, bass.ds(i * 2 + b, 1)], X[:, t, :],
                                             ALU.mult, ALU.add).then_inc(y_used[L], 1)

            def experts(L):
                dve.sem_inc(y_used[L], 5)
                with dve.Fori(0, NX // 2) as i:
                    for b in range(2):
                        add_expert(L, i, b, range(NT))
                dve.wait_ge(y_used[L], 5 + NX * NT)

            def edges():
                dve.sem_inc(onehots, 2 * NG)
                dve.memset(zeros[:, :], 0.0).then_inc(zeros_ready, 1)
                dve.wait_ge(const_in, 16)
                dve.tensor_copy(iota16, CONST(const, "iota", TP))
                dve.memset(XWE[:, :, D:D + 1], 1.0)
                dve.wait_ge(edges_in, 48)
                link(dve.tensor_copy(nodef, nodes))
                for d in range(NT):
                    ins = dve.tensor_scalar(local[:, d, :], nodef[:, 1, :], -float(d * TP), None, ALU.add)
                link(ins)
                for d in range(NT):
                    ins = dve.tensor_scalar(scratch[:, d * ET:(d + 1) * ET], local[:, d, :], 0.0, None, ALU.is_ge)
                link(ins)
                for d in range(NT):
                    dve.scalar_tensor_tensor(inside[:, d, :], local[:, d, :], float(TP),
                                             scratch[:, d * ET:(d + 1) * ET], ALU.is_lt,
                                             ALU.mult).then_inc(inside_ready, 1)
                dve.wait_ge(inside_ready, NT)
                for d in range(NT):
                    ins = dve.scalar_tensor_tensor(local[:, d, :], nodef[:, 2, :], float(TP), local[:, d, :],
                                                   ALU.mult, ALU.add)
                link(ins)
                for d in range(NT):
                    ins = dve.scalar_tensor_tensor(local[:, d, :], local[:, d, :], 1.0, inside[:, d, :],
                                                   ALU.add, ALU.mult)
                link(ins)
                link(dve.tensor_scalar(local, local, -1.0, None, ALU.add))
                dve.wait_ge(dve_full, 4)
                n["v"] = 4
                found = work[:, 0:NT * NG].rearrange("p (d g) -> p d g", d=NT)
                first, last = (work[:, (1 + j) * NT * NG:(2 + j) * NT * NG].rearrange("p (d g) -> p d g", d=NT)
                               for j in range(2))
                lim = work[:, 3 * NT * NG:3 * NT * NG + 4 * NT].rearrange("p (a d) -> p a d", a=4)
                dve.tensor_reduce(found, PS[0:1, 7, 0:NT * ET].rearrange("p (d g q) -> p d g q", d=NT, q=2), AX.X,
                                  ALU.add).then_inc(dve_free, 4)
                dve.wait_ge(dve_free, 4)
                link(dve.tensor_scalar(found, found, 0.0, None, ALU.is_gt))
                weights = CONST(const, "groups", 1).rearrange("p (a g) -> p a g", a=2)
                for j, v in enumerate((first, last)):
                    link(dve.tensor_tensor(v, found, weights[:, j:j + 1, :].broadcast_to([1, NT, NG]), ALU.mult))
                    link(dve.tensor_reduce(lim[:, j, :], v, AX.X, ALU.max))
                link(dve.tensor_scalar(lim[:, 0, :], lim[:, 0, :], 1.0, None, ALU.max))
                link(dve.tensor_scalar(lim[:, 0, :], lim[:, 0, :], -1.0, float(NG), ALU.mult, ALU.add))
                link(dve.tensor_scalar(lim[:, 3, :], lim[:, 0, :], 1.0, None, ALU.add))
                link(dve.tensor_tensor(lim[:, 1, :], lim[:, 1, :], lim[:, 3, :], ALU.max))
                link(dve.tensor_tensor(lim[:, 3, :], lim[:, 1, :], lim[:, 0, :], ALU.subtract))
                link(dve.memset(lim[:, 2, :], float(NG)))
                for d in range(1, NT):
                    link(dve.tensor_tensor(lim[:, 2, d:d + 1], lim[:, 2, d - 1:d], lim[:, 3, d - 1:d], ALU.add))
                link(dve.tensor_tensor(lim[:, 2, :], lim[:, 2, :], lim[:, 0, :], ALU.subtract))
                dve.tensor_copy(ranges[:, :], lim[:, 0:3, :].rearrange("p a d -> p (a d)")).then_inc(ranges_ready, 1)
                dve.wait_ge(ranges_ready, 1)
                for d in range(NT):
                    start = dve.value_load(ranges[0:1, d:d + 1], min_val=0, max_val=NG - 1)
                    stop = dve.value_load(ranges[0:1, NT + d:NT + d + 1], min_val=1, max_val=NG)
                    shift = dve.value_load(ranges[0:1, 2 * NT + d:2 * NT + d + 1], min_val=0, max_val=NT * NG)
                    with dve.Fori(start, stop) as i:
                        for q in range(2):
                            j = bass.ds(i * 2 + q, 1)
                            dve.wait_ge(edge_mm, shift * 2 + i * 2 + (q + 1))
                            dve.tensor_scalar(src_hot[:, q, :], iota16, nodef[:, 0, j], None, ALU.is_equal)
                            dve.tensor_scalar(dst_hot[:, q, :], iota16[:, 0:2 * TP], local[:, d, j], None,
                                              ALU.is_equal).then_inc(onehots, 1)
                    dve.wait_ge(adj_full, d + 1)
                    for r in range(2):
                        ins = dve.tensor_copy(AR[r][:, 3:NT, d * TP:(d + 1) * TP], PS[0:TP, 3:NT, r * TP:(r + 1) * TP])
                    ins.then_inc(adj_copied, 1)
                dve.wait_ge(adj_copied, NT)
                dve.wait_ge(adj_copied_act, NT)
                dve.tensor_tensor(AT[:, :, :], A0T, A1T, ALU.add).then_inc(at_ready, 1)

            def layer0_gnn():
                layer_norm(X, XN, True)
                take_transposes(XT)
                dve.wait_ge(at_ready, 1)
                sage(N, 0, True, add_to_x)
                chained()

            def layer0_attention():
                layer_norm(X, XN, False)
                rms_norm()
                take_transposes(XT, scale=COLS(cols, "ln1_w"))
                cos = CONST(const, "cos", TP).rearrange("p (t n) -> p t n", t=NT)
                sin = CONST(const, "sin", TP).rearrange("p (t n) -> p t n", t=NT)
                for t in range(NT):
                    b = bank()
                    src = PS[0:TP, b, 0:384].rearrange("p (h n) -> p h n", h=6)
                    r0 = rope[:, 0, :].rearrange("p (h n) -> p h n", h=6)
                    r1 = rope[:, 1, :].rearrange("p (h n) -> p h n", h=6)

                    def per_head(v, n0, n1):
                        return v[:, t, n0:n1].unsqueeze(1).broadcast_to([TP, 6, n1 - n0])

                    dve.tensor_tensor(r0, src, per_head(cos, 0, 64), ALU.mult)
                    dve.tensor_tensor(r1[:, :, 0:32], src[:, :, 32:64], per_head(sin, 0, 32), ALU.mult)
                    link(dve.tensor_tensor(r1[:, :, 32:64], src[:, :, 0:32], per_head(sin, 32, 64), ALU.mult))
                    taken(dve.tensor_copy(vv[:, t, :], PS[0:TP, b, 384:512]))
                    link(dve.tensor_tensor(qk[:, t, :], rope[:, 0, :], rope[:, 1, :], ALU.add))
                    dve.sem_inc(rope_ready, 1)
                for t in range(NT):
                    b = bank()
                    taken(dve.tensor_copy(qkT[:, :, t * TP:(t + 1) * TP],
                                          PS[:, b, 0:375].rearrange("p (k n) -> p k n", k=3)))
                steps = [(h, t) for h in range(4) for t in range(NT)]
                mx = col[:, 160:162]
                nmx = col[:, 162:164]
                rsum = col[:, 164:166]
                rinv = col[:, 166:168]

                def row_max(s):
                    h, t = steps[s]
                    q, base, keys = s % 2, (s % 2) * 2, (steps[s][1] + 1) * TP
                    dve.wait_ge(scores_full, s + 1)
                    link(dve.tensor_reduce(mx[:, q:q + 1], PF[0:TP, base * 512:base * 512 + keys], AX.X, ALU.max))
                    if s >= 2:
                        dve.wait_ge(probs_ready, s - 1)
                    dve.tensor_scalar(nmx[:, q:q + 1], mx[:, q:q + 1], -0.125, None,
                                      ALU.mult).then_inc(nmax_ready, 1)

                def take_turned(s):
                    h, t = steps[s]
                    q, pt = s % 2, 4 + 2 * (s % 2)
                    dve.wait_ge(pt_full, s + 1)
                    if s >= 2:
                        dve.wait_ge(y_out_full, s - 1)
                    dve.tensor_copy(pT[:, q, 0:t + 1, :], turned(pt)[:, 0:t + 1, :]).then_inc(pt_copied, 1)

                def take_output(s):
                    h, t = steps[s]
                    q, pt = s % 2, 4 + 2 * (s % 2)
                    dve.wait_ge(probs_ready, s + 1)
                    link(dve.reciprocal(rinv[:, q:q + 1], rsum[:, q:q + 1]))
                    dve.wait_ge(y_out_full, s + 1)
                    dve.tensor_scalar(attn[:, t, h * 64:(h + 1) * 64], PS[0:TP, pt + 1, 256:320], rinv[:, q:q + 1],
                                      None, ALU.mult).then_inc(y_taken, 1)

                row_max(0)
                for s in range(len(steps) + 1):
                    if s + 1 < len(steps):
                        row_max(s + 1)
                    if s < len(steps):
                        take_turned(s)
                    if s >= 1:
                        take_output(s - 1)
                take_transposes(XT)
                for t in range(NT):
                    b = bank()
                    taken(dve.tensor_tensor(XN[:, t, :], XN[:, t, :], PS[0:TP, b, 0:D], ALU.add))
                own_banks()

            def layer0_moe():
                rms_norm()
                dve.tensor_tensor(X[:, :, :], X[:, :, :], XN[:, :, :], ALU.add).then_inc(chain, 1)
                n["chain"] += 1
                take_transposes(XT, scale=COLS(cols, "ln2_w"))
                gating(0)
                chained()
                dve.sem_inc(hid_free[0], 2)
                dve.sem_inc(y_used[0], 5)
                hid = HT[:, 0:M0 * N].rearrange("p (m n) -> p m n", m=M0)
                with dve.Fori(0, NX // 2) as i:
                    for b in range(2):
                        for half, (c0, c) in enumerate(HALVES):
                            for m in range(M0):
                                mw = min(128, HID0 - m * 128)
                                ch = (b * 2 + half) * M0 + m
                                dve.wait_ge(silu_ready, i * 24 + (ch + 1))
                                dve.tensor_tensor(hid[0:mw, m, c0:c0 + c], silu[0:mw, ch % 2, 0:c],
                                                  PS[0:mw, (ch % 2) * 2 + 1, 0:c], ALU.mult).then_inc(hid_free[0], 1)
                        add_expert(0, i, b, range(NT))
                dve.wait_ge(y_used[0], 5 + NX * NT)

            def layer1_gnn():
                layer_norm(X, XN, True)
                link(dve.tensor_tensor(bsum[:, :], COLS(cols, "b_ih"), COLS(cols, "b_hh"), ALU.add))
                dve.sem_inc(bsum_ready, 1)
                take_transposes(XT)
                for r in range(2):
                    for t in range(NT):
                        b = bank()
                        taken(dve.tensor_scalar(msg[r][:, t, 0:D], PS[0:TP, b, 0:D], 0.0, None, ALU.max))
                for k in range(KD):
                    dve.wait_ge(gates_ready, 8 + 2 * k + 2)
                    dve.tensor_tensor(ST2[:, k, :], lstm[:, k, :], lstm[:, 2 + k, :], ALU.mult).then_inc(cell_in, 1)
                for k in range(KD):
                    dve.wait_ge(cell_tanh, k + 1)
                    dve.tensor_tensor(XT[:, k, :], lstm[:, 4 + k, :], ST2[:, k, :], ALU.mult).then_inc(cell_ready, 1)
                for t in range(NT):
                    b = bank()
                    taken(dve.tensor_tensor(X[:, t, :], X[:, t, :], PS[0:TP, b, 0:D], ALU.add))
                own_banks()

            def layer1_moe():
                layer_norm(X, XN, False)
                own_norm()
                layer_norm(XN, ROOT, True)
                take_transposes(XT, scale=COLS(cols, "gamma"), bias=COLS(cols, "beta"))
                gating(1)
                take_bias2()
                experts(1)

            def layer2_gnn():
                layer_norm(X, XN, True)
                take_transposes(XT)
                xh = XH.rearrange("p t (h c) -> p t h c", h=NX)
                own_norm()
                for t in range(NT):
                    dve.tensor_copy(xh[:, t, :, 0:32], XN[:, t, :].rearrange("p (c h) -> p h c", h=NX))
                    ins = dve.memset(xh[:, t, :, 32:33], 1.0)
                link(ins)
                b = bank()
                taken(dve.tensor_copy(vcol, PS[0:TP, b, 0:NT * NX].rearrange("p (t e) -> p t e", t=NT)))
                own_banks()
                dve.tensor_scalar(v02, vcol, 0.2, None, ALU.mult).then_inc(v_ready, 1)
                for d in range(NT):
                    for c0, c in ((0, 500), (500, 125)):
                        b = bank()
                        taken(dve.tensor_scalar(maskb[:, d, c0:c0 + c], PS[0:TP, b, 0:c], 0.0, NEG,
                                                ALU.is_equal, ALU.mult))
                own_banks()
                dve.wait_ge(v_ready, 1)
                umax = [col[:, 168 + 8 * j:168 + 8 * j + NT] for j in range(2)]
                emax = [col[:, 184 + 8 * j:184 + 8 * j + NT] for j in range(2)]
                nm = [col[:, 200 + 8 * j:200 + 8 * j + NT] for j in range(2)]
                den = col[:, 216:216 + NT]
                rden = col[:, 224:224 + NT]
                out_h = scratch[:, 0:NT * 32]

                def masked(h, t):
                    if t == 0:
                        dve.wait_ge(u_full, h + 1)
                    dve.tensor_tensor_reduce(raw[h % 2][:, t, :], PF[0:TP, 0:N], maskb[:, t, :],
                                             1.0, -3.0e38, ALU.add, ALU.max,
                                             umax[h % 2][:, t:t + 1]).then_inc(raw_done, 1)

                def target_max(h):
                    j = h % 2
                    dve.wait_ge(raw_done, (h + 1) * NT)
                    link(dve.tensor_tensor(emax[j], umax[j], vcol[:, :, h], ALU.add))
                    link(dve.scalar_tensor_tensor(nm[j], emax[j], 0.2, emax[j], ALU.mult, ALU.max))
                    link(dve.tensor_scalar(nm[j], nm[j], -1.0, None, ALU.mult))

                def leaky(s):
                    h, t = divmod(s, NT)
                    dve.wait_ge(z02_done, s + 1)
                    dve.scalar_tensor_tensor(zz[0:TP, s % 2, :], raw[h % 2][:, t, :], vcol[:, t, h:h + 1],
                                             zz[0:TP, s % 2, :], ALU.add, ALU.max).then_inc(z_done, 1)

                def count_edges(s):
                    t, q, pt = s % NT, s % 2, 4 + 2 * (s % 2)
                    dve.wait_ge(gat_tr, s + 1)
                    if s >= 2:
                        dve.wait_ge(gat_full, s - 1)
                    dve.tensor_tensor(pT[:, q, :, :], turned(pt), AT[:, :, t * TP:(t + 1) * TP],
                                      ALU.mult).then_inc(gat_pt, 1)

                def normalise(h):
                    y = PS[0:TP, 2 + h % 2, 0:NT * 33].rearrange("p (t c) -> p t c", t=NT)
                    o = out_h.rearrange("p (t c) -> p t c", t=NT)
                    dve.wait_ge(gat_full, (h + 1) * NT)
                    link(dve.tensor_scalar(den, y[:, :, 32], 1e-30, None, ALU.max))
                    link(dve.reciprocal(rden, den))
                    dve.tensor_tensor(o, y[:, :, 0:32], rden.unsqueeze(2).broadcast_to([TP, NT, 32]),
                                      ALU.mult).then_inc(gat_taken, 1)
                    dve.wait_ge(gat_taken, h + 1)
                    xs = X[:, :, :].rearrange("p t (c h) -> p h t c", h=NX)[:, h]
                    link(dve.tensor_tensor(xs, xs, o, ALU.add))

                for t in range(NT):
                    masked(0, t)
                target_max(0)
                for s in range(NX * NT + 3):
                    h, t = divmod(s, NT)
                    if s < NX * NT:
                        leaky(s)
                    if 1 <= s <= NX * NT:
                        count_edges(s - 1)
                    if h + 1 < NX:
                        masked(h + 1, t)
                        if t == NT - 1:
                            target_max(h + 1)
                    if h and t == 2:
                        normalise(h - 1)

            def layer2_moe():
                layer_norm(X, XN, True)
                take_transposes(XT)
                gating(2)
                link(dve.tensor_tensor(X[:, :, :], X[:, :, :], XN[:, :, :], ALU.add))
                take_bias2()
                experts(2)

            def tanh_scores(s, level):
                small, big, sign, mask = (col[:, 208 + 8 * j:208 + 8 * j + NT] for j in range(4))
                dve.tensor_copy(small, s)
                link(dve.scalar_tensor_tensor(mask, s, -1.0, s, ALU.mult, ALU.max))
                dve.tensor_copy(big, mask).then_inc(tanh_in, 1)
                link(dve.tensor_scalar(mask, mask, 4.0, None, ALU.is_lt))
                link(dve.tensor_scalar(sign, s, 0.0, 2.0, ALU.is_ge, ALU.mult))
                link(dve.tensor_scalar(sign, sign, -1.0, None, ALU.add))
                dve.wait_ge(tanh_out, 2 * (level + 1))
                link(dve.tensor_scalar(big, big, 1.0, None, ALU.add))
                link(dve.reciprocal(s, big))
                link(dve.tensor_scalar(s, s, 2.0, -1.0, ALU.mult, ALU.add))
                link(dve.tensor_tensor(s, s, sign, ALU.mult))
                link(dve.tensor_tensor(small, small, mask, ALU.mult))
                link(dve.tensor_scalar(mask, mask, -1.0, 1.0, ALU.mult, ALU.add))
                link(dve.tensor_tensor(s, s, mask, ALU.mult))
                link(dve.tensor_tensor(s, s, small, ALU.add))

            def layer3_gnn():
                layer_norm(X, XN, True)
                score = col[:, 168:168 + NT]
                rank = col[:, 176:176 + NT]
                tie = [col[:, 184 + 8 * j:184 + 8 * j + NT] for j in range(2)]
                wn = col[:, 200:202]
                unread = ST[0:TP, 0, :]
                for i in range(3):
                    rows_, kept = LEVELS[i], LEVELS[i + 1]
                    ts, ks = tiles(rows_), tiles(kept)
                    take_transposes(XT if i == 0 else XLT[i], rows_)
                    sage(rows_, i, i > 0, relu_root)
                    take_transposes(ST, rows_)
                    sage(rows_, i, False, lambda t, c: None)
                    pw = poolw[:, i * D:(i + 1) * D]
                    link(dve.tensor_tensor_reduce(scratch[:, 0:D], pw, pw, 1.0, 0.0, ALU.mult, ALU.add, wn[:, 0:1]))
                    link(dve.memset(score, 0.0))
                    for t, c0, c in ts:
                        ins = dve.tensor_tensor_reduce(XWE[0:c, t, 0:D], ROOT[0:c, t, :], pw[0:c, :], 1.0, 0.0,
                                                       ALU.mult, ALU.add, score[0:c, t:t + 1])
                    link(ins)
                    link(dve.tensor_copy(col[:, 0:NT], wn[:, 0:1].broadcast_to([TP, NT])))
                    rstd(dve.tensor_copy(col[:, 0:1], wn[:, 0:1]))
                    link(dve.tensor_scalar(score, score, col[:, 8:9], None, ALU.mult))
                    tanh_scores(score, i)
                    for t, c0, c in ts:
                        ins = dve.tensor_scalar(diag[:, t, :], ident[0:TP, 0:TP], score[:, t:t + 1], None, ALU.mult)
                    ins.then_inc(diag_ready, 1)
                    for t, c0, c in ts:
                        ins = dve.tensor_scalar(ROOT[0:c, t, :], ROOT[0:c, t, :], score[0:c, t:t + 1], None, ALU.mult)
                    link(ins)
                    for part in (ts[:4], ts[4:]):
                        if part:
                            c0, c1 = part[0][1], part[-1][1] + part[-1][2]
                            b = bank()
                            taken(dve.tensor_copy(scoreb[:, c0:c1], PS[0:TP, b, 0:c1 - c0]))
                    own_banks()
                    link(dve.memset(tie[0], 0.0))
                    for t, c0, c in ts:
                        link(dve.tensor_scalar(unread[0:c, 0:rows_], scoreb[0:c, 0:rows_], score[0:c, t:t + 1], 0.0,
                                               ALU.is_gt, ALU.add, accum_out=rank[0:c, t:t + 1]))
                        if c0:
                            link(dve.tensor_scalar(unread[0:c, 0:c0], scoreb[0:c, 0:c0], score[0:c, t:t + 1], 0.0,
                                                   ALU.is_equal, ALU.add, accum_out=tie[0][0:c, t:t + 1]))
                        link(dve.scalar_tensor_tensor(unread[0:c, 0:c], scoreb[0:c, c0:c0 + c], score[0:c, t:t + 1],
                                                      CONST(const, "before", TP)[0:c, 0:c], ALU.is_equal, ALU.mult,
                                                      accum_out=tie[1][0:c, t:t + 1]))
                    for t, c0, c in ts:
                        ins = dve.tensor_tensor(rank[0:c, t:t + 1], rank[0:c, t:t + 1], tie[0][0:c, t:t + 1], ALU.add)
                    link(ins)
                    for t, c0, c in ts:
                        ins = dve.tensor_tensor(rank[0:c, t:t + 1], rank[0:c, t:t + 1], tie[1][0:c, t:t + 1], ALU.add)
                    link(ins)
                    for t, c0, c in ts:
                        ins = dve.tensor_scalar(PT[0:c, t, 0:kept], CONST(const, "iota", TP)[0:c, 0:kept],
                                                rank[0:c, t:t + 1], None, ALU.is_equal)
                    ins.then_inc(perm_ready, 1)
                    for kt, k0, kc in ks:
                        b = bank()
                        taken(dve.tensor_copy(XL[i + 1][0:kc, kt, :], PS[0:kc, b, 0:D]))
                        own_banks()
                        if i < 2:
                            dve.sem_inc(xn_ready, 1)
                dve.memset(CMT, 0.0).then_inc(cmt_cleared, 1)
                for i in (1, 0):
                    ts = tiles(LEVELS[i])
                    for t, c0, c in ts:
                        b = bank()
                        taken(dve.tensor_scalar(ROOT[0:c, t, :], PS[0:c, b, 0:D], 0.0, None, ALU.max))
                    take_transposes(ST, LEVELS[i])
                    for t, c0, c in ts:
                        b = bank()
                        if i:
                            taken(dve.tensor_copy(XN[0:c, t, :], PS[0:c, b, 0:D]))
                        else:
                            taken(dve.tensor_tensor(X[0:c, t, :], X[0:c, t, :], PS[0:c, b, 0:D], ALU.add))
                    if i:
                        dve.sem_inc(cmt_cleared, 1)
                own_banks()

            def layer3_moe():
                layer_norm(X, XN, True)
                take_transposes(XT)
                gating(3)
                take_bias2()
                experts(3)

            def own_norm():
                link(dve.tensor_copy(col[:, 16:17], col[:, 0:1]))

            edges()
            dve.wait_ge(x_in, 16)
            dve.wait_ge(small_in, 16 * 7)
            layer0_gnn()
            layer0_attention()
            layer0_moe()
            layer1_gnn()
            layer1_moe()
            layer2_gnn()
            layer2_moe()
            layer3_gnn()
            layer3_moe()
            dve.sem_inc(layer_done, 1)

        @block.scalar
        def _(act):
            n = {"a": 0, "exp": 0}

            def bank():
                n["a"] += 1
                act.wait_ge(act_full, n["a"])
                return (n["a"] - 1) % 4

            def take_transposes(dst, rows_=N, scale=None, bias=None):
                ts = tiles(rows_)
                for part in (ts[:4], ts[4:]):
                    if not part:
                        continue
                    c0, c1 = part[0][1], part[-1][1] + part[-1][2]
                    b = bank()
                    act.activation(dst[:, 1, c0:c1], PS[:, b, 0:c1 - c0], ACT.Identity,
                                   scale=1.0 if scale is None else scale[:, 1:2],
                                   bias=0.0 if bias is None else bias[:, 1:2]).then_inc(act_free, 1)

            def take_root(rows_):
                for t, c0, c in tiles(rows_):
                    b = bank()
                    act.activation(ROOT[0:c, t, :], PS[0:c, b, 0:D], ACT.Copy).then_inc(act_free, 1)
                    act.wait_ge(act_free, n["a"])
                    act.sem_inc(root_ready, 1)

            def feature_major(m_blocks, func, dst, bias):
                for m in range(m_blocks):
                    for c0, c in HALVES:
                        b = bank()
                        act.activation(dst(m)[:, c0:c0 + c], PS[:, b, 0:c], func, bias=bias(m)).then_inc(act_free, 1)

            def gating(L):
                act.wait_ge(logit_ready, L + 1)
                act.activation(gate[:, 1], gate[:, 1], ACT.Exp).then_inc(exp_ready, 1)

            def edges():
                for d in range(NT):
                    act.wait_ge(adj_full, d + 1)
                    for r in range(2):
                        ins = act.activation(AR[r][:, 0:3, d * TP:(d + 1) * TP], PS[0:TP, 0:3, r * TP:(r + 1) * TP],
                                             ACT.Copy)
                    ins.then_inc(adj_copied_act, 1)

            def layer0_gnn():
                act.wait_ge(small_in, 16 * 7)
                take_transposes(XT)
                take_root(N)

            def layer0_attention():
                take_transposes(XT, scale=COLS(cols, "ln1_w"))
                rsum = col[:, 164:166]
                nmx = col[:, 162:164]
                for s in range(4 * NT):
                    q, base, keys = s % 2, (s % 2) * 2, (s % NT + 1) * TP
                    act.wait_ge(nmax_ready, s + 1)
                    if s >= 2:
                        act.wait_ge(pt_full, s - 1)
                        act.wait_ge(y_taken, s - 1)
                    act.activation(probs[:, q, 0:keys], PF[0:TP, base * 512:base * 512 + keys], ACT.Exp,
                                   bias=nmx[:, q:q + 1], scale=0.125,
                                   accum_out=rsum[:, q:q + 1]).then_inc(probs_ready, 1)
                take_transposes(XT)

            def layer0_moe():
                take_transposes(XT, scale=COLS(cols, "ln2_w"))
                gating(0)
                with act.Fori(0, NX // 2) as i:
                    for b in range(2):
                        for half, (c0, c) in enumerate(HALVES):
                            for m in range(M0):
                                mw = min(128, HID0 - m * 128)
                                ch = (b * 2 + half) * M0 + m
                                act.wait_ge(hid_full[0], i * 24 + (ch + 1))
                                act.wait_ge(hid_free[0], i * 24 + (ch + 1))
                                act.activation(silu[0:mw, ch % 2, 0:c], PS[0:mw, (ch % 2) * 2, 0:c],
                                               ACT.Silu).then_inc(silu_ready, 1)

            def layer1_gnn():
                take_transposes(XT)
                act.wait_ge(bsum_ready, 1)
                for r in range(2):
                    feature_major(KD, ACT.Relu, lambda m: ST[:, m, :],
                                  lambda m: COLS(cols, "b_rel")[:, r * KD + m:r * KD + m + 1])
                feature_major(KD, ACT.Identity, lambda m: ST[:, m, :], lambda m: 0.0)
                for m in range(6):
                    for c0, c in HALVES:
                        b = bank()
                        act.activation(lstm[:, m, c0:c0 + c], PS[:, b, 0:c], ACT.Tanh if m in (2, 3) else ACT.Sigmoid,
                                       bias=bsum[:, m:m + 1]).then_inc(act_free, 1)
                        act.wait_ge(act_free, n["a"])
                        act.sem_inc(gates_ready, 1)
                for k in range(KD):
                    act.wait_ge(cell_in, k + 1)
                    act.activation(ST2[:, k, :], ST2[:, k, :], ACT.Tanh).then_inc(cell_tanh, 1)
                feature_major(1, ACT.Relu, lambda m: ST[:, 0, :], lambda m: COLS(cols, "g_b1"))
                feature_major(1, ACT.Relu, lambda m: ST[:, 1, :], lambda m: COLS(cols, "g_b2"))

            def hidden(L, blocks, at):
                hid = HT[:, 0:blocks * N].rearrange("p (m n) -> p m n", m=blocks)
                act.sem_inc(hid_free[L], 4)
                with act.Fori(0, NX // 2) as i:
                    for b in range(2):
                        for half, (c0, c) in enumerate(HALVES):
                            for m in range(blocks):
                                ch = (b * 2 + half) * blocks + m
                                act.wait_ge(hid_full[L], i * (4 * blocks) + (ch + 1))
                                act.activation(hid[:, m, c0:c0 + c], PS[:, ch % 4, 0:c], ACT.Gelu,
                                               bias=ring[:, b, at + m:at + m + 1]).then_inc(hid_free[L], 1)

            def layer1_moe():
                take_transposes(XT, scale=COLS(cols, "gamma"), bias=COLS(cols, "beta"))
                gating(1)
                hidden(1, 4, KD * 512 + 4 * D)

            def layer2_gnn():
                take_transposes(XT)
                for c0, c in HALVES:
                    b = bank()
                    act.activation(uT[:, c0:c0 + c], PS[0:NX, b, 0:c], ACT.Identity,
                                   bias=COLS(cols, "b_u", NX)).then_inc(act_free, 1)
                act.wait_ge(v_ready, 1)

                def scaled(s):
                    h, t = divmod(s, NT)
                    act.wait_ge(raw_done, s + 1)
                    if s >= 2:
                        act.wait_ge(gat_exp, s - 1)
                    act.activation(zz[0:TP, s % 2, :], raw[h % 2][:, t, :], ACT.Identity, scale=0.2,
                                   bias=v02[:, t, h:h + 1]).then_inc(z02_done, 1)

                scaled(0)
                for s in range(NX * NT):
                    h, t = divmod(s, NT)
                    if s + 1 < NX * NT:
                        scaled(s + 1)
                    act.wait_ge(z_done, s + 1)
                    if s >= 2:
                        act.wait_ge(gat_tr, s - 1)
                    act.activation(ex[:, s % 2, :], zz[0:TP, s % 2, :], ACT.Exp,
                                   bias=col[:, 200 + 8 * (h % 2) + t:201 + 8 * (h % 2) + t]).then_inc(gat_exp, 1)

            def layer2_moe():
                take_transposes(XT)
                gating(2)
                hidden(2, 2, KD * D + 2 * D)

            def layer3_gnn():
                for i in range(3):
                    rows_, kept = LEVELS[i], LEVELS[i + 1]
                    take_transposes(XT if i == 0 else XLT[i], rows_)
                    take_root(rows_)
                    take_transposes(ST, rows_)
                    take_root(rows_)
                    act.wait_ge(tanh_in, i + 1)
                    act.activation(col[:, 208:208 + NT], col[:, 208:208 + NT], ACT.Tanh).then_inc(tanh_out, 1)
                    act.activation(col[:, 216:216 + NT], col[:, 216:216 + NT], ACT.Exp,
                                   scale=-2.0).then_inc(tanh_out, 1)
                    if i < 2:
                        for t, c0, c in tiles(rows_):
                            b = bank()
                            act.activation(BM[0:c, t, 0:kept], PS[0:c, b, 0:kept], ACT.Copy).then_inc(act_free, 1)
                        for kt, k0, kc in tiles(kept):
                            b = bank()
                            act.activation(ADJ[i + 1][0:kc, kt, :], PS[0:kc, b, 0:kept],
                                           ACT.Copy).then_inc(act_free, 1)
                small = LEVELS[3]
                for i in (1, 0):
                    for which in range(2):
                        for k in range(KD):
                            b = bank()
                            act.activation(CMT[:, k, 0:small], PS[:, b, 0:small], ACT.Copy).then_inc(act_free, 1)
                        if which == 0:
                            take_transposes(ST, LEVELS[i])
                    small = LEVELS[i]

            def layer3_moe():
                take_transposes(XT)
                hid = HT[:, :].rearrange("p (m n) -> p m n", m=8)
                feature_major(8, ACT.Gelu, lambda m: hid[:, m, :], lambda m: COLS(cols, "l3_b1")[:, m:m + 1])
                gating(3)

            edges()
            layer0_gnn()
            layer0_attention()
            layer0_moe()
            layer1_gnn()
            layer1_moe()
            layer2_gnn()
            layer2_moe()
            layer3_gnn()
            layer3_moe()

        @block.gpsimd
        def _(pool):
            pool.memset(power[:, :], -0.5).then_inc(power_set, 1)
            pool.wait_ge(power_set, 1)
            for j in range(NORMS):
                pool.wait_ge(var_ready, j + 1)
                pool.tensor_tensor(col[:, 8:8 + NT], col[:, 0:NT], power[:, :], ALU.pow).then_inc(rstd_ready, 1)

        @block.sync
        def _(sp):
            sp.dma_start(const[:, :], io["const"]).then_inc(const_in, 16)
            sp.dma_start(nodes[:, 0, :], io["src"]).then_inc(edges_in, 16)
            sp.dma_start(nodes[:, 1, :], io["dst"]).then_inc(edges_in, 16)
            sp.dma_start(nodes[:, 2, :], io["etype"]).then_inc(edges_in, 16)
            sp.dma_start(X[:, :, :], io["x"]).then_inc(x_in, 16)
            for dst, name in ((w0[:, 0:W0.size], "w0"), (rows[:, :], "rows"), (cols[:, :], "cols"), (w1[:, :], "w1"),
                              (wr[:, :], "wr"), (b2s[:, :], "b2s")):
                sp.dma_start(dst, io[name]).then_inc(small_in, 16)
            sp.dma_start(poolw[:, :], io["poolw"].broadcast_to([TP, 3 * D])).then_inc(small_in, 16)

            def experts(L, size):

                def load(e, b):
                    sp.dma_start(ring[:, b, 0:size],
                                 io[f"experts{L}"][bass.ds(e, 1), :, :].rearrange("a p n -> p (a n)")
                                 ).then_inc(slot_in[b], 16)

                if L:
                    sp.wait_ge(y_full[L - 1], NX * NT)
                for b in range(2):
                    load(b, b)
                with sp.Fori(1, NX // 2) as i:
                    for b in range(2):
                        sp.wait_ge(y_full[L], i * 10 + (5 * b - 5))
                        load(i * 2 + b, b)

            experts(0, SLOT0)
            experts(1, KD * 512 + 4 * D + 4)
            sp.wait_ge(gnn_weights_used, 2)
            experts(2, KD * D + 2 * D + 2)
            sp.dma_start(arena[:, 0:WG.size], io["gnn3"]).then_inc(gnn3_in, 16)
            sp.dma_start(rows3, io["rows3"]).then_inc(gnn3_in, 16)
            sp.dma_start(w0[:, 0:KD * 1024], io["w1_3"]).then_inc(w1_3_in, 16)
            experts(3, 8 * D)
            sp.wait_ge(layer_done, 1)
            sp.dma_start(out, X[:, :, :]).then_inc(out_done, 16)
            sp.wait_ge(out_done, 16)


def constants():
    c = np.zeros((128, CONST.size), np.float32)

    def put(name, value):
        a, w = CONST.at[name]
        value = np.asarray(value, np.float32)
        value = value.reshape(value.shape[0], -1)
        c[0:value.shape[0], a:a + w] = value

    put("ident", np.eye(128))
    put("ones", np.ones((128, 128)))
    put("iota", np.tile(np.arange(626), (128, 1)))
    inv_freq = 1.0 / 10000.0 ** (np.arange(0, 64, 2, dtype=np.float32) / 64)
    freqs = np.outer(np.arange(N, dtype=np.float32), inv_freq)
    emb = np.concatenate([freqs, freqs], axis=-1)
    sign = np.concatenate([-np.ones(32), np.ones(32)])
    put("cos", np.cos(emb).reshape(NT, TP, 64).transpose(1, 0, 2))
    put("sin", (np.sin(emb) * sign).reshape(NT, TP, 64).transpose(1, 0, 2))
    i = np.arange(TP)
    put("causal", np.where(i[None, :] > i[:, None], NEG, 0.0))
    put("before", i[None, :] < i[:, None])
    e = np.arange(NX)
    put("before8", np.tile((e[None, :] < e[:, None]).reshape(1, -1), (128, 1)))
    g = np.arange(NG)
    put("groups", np.tile(np.concatenate([NG - g, g + 1]), (128, 1)))
    r = np.arange(3 * TP)
    cm = (r[:, None] <= r[None, :313]) / (r[None, :313] + 1.0)
    put("cummean", cm.reshape(3, TP, 313).transpose(1, 0, 2))
    return c


def kernel(**inputs):
    import concourse.bacc as bacc
    from concourse.bass_utils import run_bass_kernel_spmd as run

    a = {k: np.ascontiguousarray(v) for k, v in inputs.items()}

    def part(w):
        return w.reshape(-1, 128, w.shape[-1]).transpose(1, 0, 2).reshape(128, -1)

    def column(v):
        return v.reshape(-1, 128).T

    def pack(*parts_):
        return np.ascontiguousarray(np.concatenate(parts_, axis=-1))

    def row(v):
        return v.reshape(1, -1)

    wq = a["L0_ffn_wq"].reshape(4, 64, D)[[0, 2, 1, 3]].reshape(D, D)
    wqkv = np.concatenate([wq.T, a["L0_ffn_wk"].T, a["L0_ffn_wv"].T], axis=1)
    gates = [slice(0, D), slice(2 * D, 3 * D), slice(3 * D, 4 * D)]
    w_ih = np.concatenate([a["L1_gnn_W_ih"][g] for g in gates]).T
    b_ih, b_hh = (np.concatenate([a[f"L1_gnn_{b}"][g] for g in gates]) for b in ("b_ih", "b_hh"))
    pad = M0 * 128 - HID0
    w2t = np.concatenate([a["L0_ffn_w2"].transpose(0, 2, 1), np.zeros((NX, pad, D), np.float32)], axis=1)
    b_u = np.zeros((128, 1), np.float32)
    b_u[0:NX, 0] = a["L2_gnn_b_u"]
    pre = "L3_gnn_"
    host = {
        "const": constants(),
        **{name: np.ascontiguousarray(a[key].reshape(ET, TP).T)
           for name, key in (("src", "src"), ("dst", "dst"), ("etype", "edge_type_2"))},
        "x": np.ascontiguousarray(a["x"].reshape(NT, TP, D).transpose(1, 0, 2)),
        "rows": pack(row(a["L0_gnn_b_r"]), row(a["L1_gnn_b_rel"]), row(a["L1_gnn_b3"]), row(a["L1_ffn_br"])),
        "rows3": pack(*[row(a[pre + f"db{k}"][i]) for i in range(3) for k in (1, 2)],
                     *[row(a[pre + f"ub{k}"][i]) for i in range(2) for k in (1, 2)], row(a["L3_ffn_bg"])),
        "cols": pack(column(a["L0_ffn_ln1_w"]), column(a["L0_ffn_ln2_w"]), column(a["L1_gnn_b_rel"]),
                     column(b_ih), column(b_hh), column(a["L1_gnn_b1"]), column(a["L1_gnn_b2"]),
                     column(a["L1_ffn_gamma"]), column(a["L1_ffn_beta"]), column(a["L3_ffn_b1"]), b_u),
        "w0": pack(part(a["L0_gnn_W_l"].T), part(a["L0_gnn_W_r"].T), part(wqkv), part(a["L0_ffn_wo"].T),
                   part(a["L0_ffn_router_w"].T)),
        "w1": pack(part(a["L1_gnn_W_rel"][0].T), part(a["L1_gnn_W_rel"][1].T), part(w_ih), part(a["L1_gnn_W1"].T),
                   part(a["L1_gnn_W2"].T), part(a["L1_gnn_W3"].T)),
        "wr": pack(part(a["L1_ffn_Wr"]), part(a["L2_ffn_router_w"].T), part(a["L3_ffn_Wg"]),
                   part(a["L2_gnn_W_u"].T), part(a["L2_gnn_W_v"].T)),
        "b2s": pack(a["L1_ffn_b2"], a["L2_ffn_b2"], a["L3_ffn_bd"]),
        "poolw": a["L3_gnn_pool_w"].reshape(1, 3 * D),
        "gnn3": pack(*[part(a[pre + f"dW{m}{k}"][i].T) for i in range(3) for k in (1, 2) for m in "lr"],
                     *[part(a[pre + f"uW{m}{k}"][i].T) for i in range(2) for k in (1, 2) for m in "lr"]),
        "w1_3": part(a["L3_ffn_W1"]),
        "experts0": np.stack([pack(part(a["L0_ffn_w1"][e].T), part(a["L0_ffn_w3"][e].T), part(w2t[e]))
                              for e in range(NX)]),
        "experts1": np.stack([pack(part(a["L1_ffn_W1"][e]), part(a["L1_ffn_W2"][e]), column(a["L1_ffn_b1"][e])) for e in range(NX)]),
        "experts2": np.stack([pack(part(a["L2_ffn_w1"][e]), part(a["L2_ffn_w2"][e]), column(a["L2_ffn_b1"][e])) for e in range(NX)]),
        "experts3": np.stack([part(a["L3_ffn_Wd"][e]) for e in range(NX)]),
    }
    nc = bacc.Bacc("TRN2", target_bir_lowering=False, num_devices=1)
    arrays, io = {}, {}
    for name, v in host.items():
        arrays[f"in_{name}"] = np.ascontiguousarray(v)
        io[name] = nc.dram_tensor(f"in_{name}", v.shape, mybir.dt.from_np(v.dtype), kind="ExternalInput").ap()
    out = nc.dram_tensor("out", (N, D), F32, kind="ExternalOutput").ap()
    build(nc, io, out.rearrange("(t p) d -> p t d", t=NT))
    return run(nc, [arrays], core_ids=[0]).results[0]["out"]
```
